# Optimizing a Trainium2 kernel written in Bass

```python
import numpy as np
import jax
import jax.numpy as jnp

def _softmax(x, axis=-1):
    return jax.nn.softmax(x, axis=axis)

def _gelu(x):
    return jax.nn.gelu(x, approximate=True)

def _silu(x):
    return jax.nn.silu(x)

def _sigmoid(x):
    return jax.nn.sigmoid(x)

def _layernorm(x, axis=-1, eps=1e-05):
    m = jnp.mean(x, axis=axis, keepdims=True)
    v = jnp.var(x, axis=axis, keepdims=True)
    return (x - m) / jnp.sqrt(v + eps)

def _scatter_add(tgt, idx, src, axis=0):
    return tgt.at[idx].add(src)

def _segment_sum(src, seg, n):
    return jax.ops.segment_sum(src, seg, n)
kernel_name = 'mk_adaln_d1_jaxref_r8_506a92'

def setup_inputs(seed: int=0):
    np.random.seed(seed)
    _w = jnp.asarray

    def _L0_attn_setup():
        import jax, jax.numpy as jnp
        import numpy as np
        EMBED = 128
        H = 16
        KV = 4
        D = 64
        K_NODES = 4
        TOP_K = 2
        MAXLEN = 1024
        BASE = 10000.0
        SCALE = D ** (-0.5)
        NEG = -1000000000.0

        def _rotate_half(t):
            h = t.shape[-1] // 2
            return jnp.concatenate([-t[..., h:], t[..., :h]], axis=-1)

        def _rope_cache():
            inv_freq = 1.0 / BASE ** (jnp.arange(0, D, 2, dtype=jnp.float32) / D)
            t = jnp.arange(MAXLEN, dtype=jnp.float32)
            freqs = t[:, None] * inv_freq[None, :]
            emb = jnp.concatenate([freqs, freqs], axis=-1)
            return (jnp.cos(emb), jnp.sin(emb))
        key = jax.random.key(seed)
        ks = jax.random.split(key, 6)
        B, N = (1, 256)
        x = jax.random.normal(ks[0], (B, N, EMBED), jnp.float32)
        wq = 0.02 * jax.random.normal(ks[1], (EMBED, H * D), jnp.float32)
        wk = 0.02 * jax.random.normal(ks[2], (EMBED, KV * D), jnp.float32)
        wv = 0.02 * jax.random.normal(ks[3], (EMBED, KV * D), jnp.float32)
        wr = 0.02 * jax.random.normal(ks[4], (EMBED, H * K_NODES), jnp.float32)
        wo = 0.02 * jax.random.normal(ks[5], (H * D, EMBED), jnp.float32)
        return {'x': x, 'wq': wq, 'wk': wk, 'wv': wv, 'wr': wr, 'wo': wo}
    _L0_attn_in = _L0_attn_setup()

    def _L0_ffn_setup():
        import jax, jax.numpy as jnp
        import numpy as np
        DIM = 128
        HID = 512
        E = 8
        TOPK = 2
        ALPHA = 2.0
        B, T = (1, 256)
        DOWN_SCALE = 0.01
        key = jax.random.key(seed)
        ks = jax.random.split(key, 8)
        s = 1.0 / np.sqrt(DIM)
        sh = 1.0 / np.sqrt(HID)
        return {'x': jax.random.normal(ks[0], (B, T, DIM), jnp.float32), 'w_router': jax.random.uniform(ks[1], (DIM, E), jnp.float32, -s, s), 'w_up': jax.random.uniform(ks[2], (E - 1, DIM, HID), jnp.float32, -s, s), 'w_gate': jax.random.uniform(ks[3], (E - 1, DIM, HID), jnp.float32, -s, s), 'w_down': jax.random.normal(ks[4], (E - 1, HID, DIM), jnp.float32) * DOWN_SCALE, 'ws_up': jax.random.uniform(ks[5], (DIM, HID), jnp.float32, -s, s), 'ws_gate': jax.random.uniform(ks[6], (DIM, HID), jnp.float32, -s, s), 'ws_down': jax.random.normal(ks[7], (HID, DIM), jnp.float32) * DOWN_SCALE}
    _L0_ffn_in = _L0_ffn_setup()
    _L0_c = _w((lambda *s: np.random.randn(*s).astype(np.float32) * 0.05)(4, 128))
    _L0_wmod = _w((lambda *s: np.random.randn(*s).astype(np.float32) * 0.05)(128, 6 * 128) * 128 ** (-0.5))
    _d = {'L0_attn_x': _L0_attn_in['x'], 'L0_attn_wq': _L0_attn_in['wq'], 'L0_attn_wk': _L0_attn_in['wk'], 'L0_attn_wv': _L0_attn_in['wv'], 'L0_attn_wr': _L0_attn_in['wr'], 'L0_attn_wo': _L0_attn_in['wo'], 'L0_ffn_w_router': _L0_ffn_in['w_router'], 'L0_ffn_w_up': _L0_ffn_in['w_up'], 'L0_ffn_w_gate': _L0_ffn_in['w_gate'], 'L0_ffn_w_down': _L0_ffn_in['w_down'], 'L0_ffn_ws_up': _L0_ffn_in['ws_up'], 'L0_ffn_ws_gate': _L0_ffn_in['ws_gate'], 'L0_ffn_ws_down': _L0_ffn_in['ws_down'], 'L0_c': _L0_c, 'L0_wmod': _L0_wmod}
    _x0 = _d['L0_attn_x']
    _d['L0_attn_x'] = jax.random.normal(jax.random.fold_in(jax.random.key(seed), 1), (4, 512, 128), dtype=_x0.dtype)
    del _x0
    return _d

def reference(L0_attn_x, L0_attn_wq, L0_attn_wk, L0_attn_wv, L0_attn_wr, L0_attn_wo, L0_ffn_w_router, L0_ffn_w_up, L0_ffn_w_gate, L0_ffn_w_down, L0_ffn_ws_up, L0_ffn_ws_gate, L0_ffn_ws_down, L0_c, L0_wmod):

    def _L0_attn_ref(x, wq, wk, wv, wr, wo):
        import jax, jax.numpy as jnp
        import numpy as np
        EMBED = 128
        H = 16
        KV = 4
        D = 64
        K_NODES = 4
        TOP_K = 2
        MAXLEN = 1024
        BASE = 10000.0
        SCALE = D ** (-0.5)
        NEG = -1000000000.0

        def _rotate_half(t):
            h = t.shape[-1] // 2
            return jnp.concatenate([-t[..., h:], t[..., :h]], axis=-1)

        def _rope_cache():
            inv_freq = 1.0 / BASE ** (jnp.arange(0, D, 2, dtype=jnp.float32) / D)
            t = jnp.arange(MAXLEN, dtype=jnp.float32)
            freqs = t[:, None] * inv_freq[None, :]
            emb = jnp.concatenate([freqs, freqs], axis=-1)
            return (jnp.cos(emb), jnp.sin(emb))
        B, N, _ = x.shape
        G = H // KV
        q = (x @ wq).reshape(B, N, H, D).transpose(0, 2, 1, 3)
        k = (x @ wk).reshape(B, N, KV, D).transpose(0, 2, 1, 3)
        v = (x @ wv).reshape(B, N, KV, D).transpose(0, 2, 1, 3)
        k = jnp.repeat(k, G, axis=1)
        v = jnp.repeat(v, G, axis=1)
        logits = (x @ wr).reshape(B, N, H, K_NODES).transpose(0, 2, 1, 3)
        tk_vals, tk_idx = jax.lax.top_k(logits, TOP_K)
        tk_w = jax.nn.softmax(tk_vals, axis=-1)
        member = jax.nn.one_hot(tk_idx, K_NODES, dtype=jnp.float32).sum(axis=-2) > 0
        m_i = member.astype(jnp.int32)
        pos = jnp.cumsum(m_i, axis=2) - m_i
        cos_c, sin_c = _rope_cache()
        causal = jnp.tril(jnp.ones((N, N), dtype=bool))
        outs = []
        for n in range(K_NODES):
            p = pos[..., n]
            c = cos_c[p]
            s = sin_c[p]
            qr = q * c + _rotate_half(q) * s
            kr = k * c + _rotate_half(k) * s
            scores = jnp.einsum('bhid,bhjd->bhij', qr, kr) * SCALE
            mk = member[..., n][:, :, None, :]
            scores = jnp.where(causal[None, None] & mk, scores, NEG)
            probs = jax.nn.softmax(scores, axis=-1)
            outs.append(jnp.einsum('bhij,bhjd->bhid', probs, v))
        outs = jnp.stack(outs, axis=3)
        gathered = jnp.take_along_axis(outs, tk_idx[..., None], axis=3)
        y = (tk_w[..., None] * gathered).sum(axis=3)
        y = y.transpose(0, 2, 1, 3).reshape(B, N, H * D)
        return y @ wo

    def _L0_ffn_ref(x, w_router, w_up, w_gate, w_down, ws_up, ws_gate, ws_down):
        import jax, jax.numpy as jnp
        import numpy as np
        DIM = 128
        HID = 512
        E = 8
        TOPK = 2
        ALPHA = 2.0
        B, T = (1, 256)
        DOWN_SCALE = 0.01
        logits = x @ w_router
        probs = jax.nn.softmax(logits.astype(jnp.float32), axis=-1).astype(logits.dtype)
        topk_vals, topk_idx = jax.lax.top_k(probs, TOPK)
        up = jnp.einsum('btd,edh->ebth', x, w_up)
        gate = jax.nn.silu(jnp.einsum('btd,edh->ebth', x, w_gate))
        exp_out = jnp.einsum('ebth,ehd->ebtd', up * gate, w_down)
        out = jnp.zeros_like(x)
        eids = jnp.arange(E - 1)
        for i in range(TOPK - 1):
            idx_i = topk_idx[..., i]
            sel = (idx_i[None, :, :] == eids[:, None, None]).astype(x.dtype)
            gathered = jnp.einsum('ebt,ebtd->btd', sel, exp_out)
            out = out + ALPHA * topk_vals[..., i:i + 1] * gathered
        shared = x @ ws_up * jax.nn.silu(x @ ws_gate) @ ws_down
        return out + shared
    x = L0_attn_x
    mod = (_silu(L0_c) @ L0_wmod).reshape(L0_c.shape[0], 6, 1, -1)
    sa, ca, ga, sb, cb, gb = (mod[:, 0], mod[:, 1], mod[:, 2], mod[:, 3], mod[:, 4], mod[:, 5])
    ga = (2 * (ga >= 0) - 1) * jnp.maximum(jnp.abs(ga), 0.25)
    gb = (2 * (gb >= 0) - 1) * jnp.maximum(jnp.abs(gb), 0.25)
    h = _layernorm(x, axis=-1) * (1 + ca) + sa
    x = x + ga * _L0_attn_ref(h, L0_attn_wq, L0_attn_wk, L0_attn_wv, L0_attn_wr, L0_attn_wo)
    h = _layernorm(x, axis=-1) * (1 + cb) + sb
    x = x + gb * _L0_ffn_ref(h, L0_ffn_w_router, L0_ffn_w_up, L0_ffn_w_gate, L0_ffn_w_down, L0_ffn_ws_up, L0_ffn_ws_gate, L0_ffn_ws_down)
    return x

_drawn_inputs = setup_inputs


def setup_inputs(seed=0):
    import zlib

    import numpy as np

    out = dict(_drawn_inputs(seed))
    spreads = {}
    factors = {'L0_attn_wq': 8.0,
     'L0_attn_wk': 8.0,
     'L0_attn_wv': 8.0,
     'L0_attn_wr': 8.0,
     'L0_attn_wo': 8.0,
     'L0_ffn_w_router': 8.0,
     'L0_ffn_w_up': 8.0,
     'L0_ffn_w_gate': 8.0,
     'L0_ffn_w_down': 8.0,
     'L0_ffn_ws_up': 5.525,
     'L0_ffn_ws_gate': 5.678,
     'L0_ffn_ws_down': 5.49,
     'L0_c': 4.473,
     'L0_wmod': 4.666}
    for name, (base, spread) in spreads.items():
        noise = np.random.default_rng([zlib.crc32(name.encode()), seed]).standard_normal(out[name].shape)
        drawn = base * np.exp(spread * noise) if base else spread * noise
        out[name] = jnp.asarray(drawn.astype(out[name].dtype))
    for name, factor in factors.items():
        out[name] = (out[name] * factor).astype(out[name].dtype)
    return out
```

```python
from contextlib import ExitStack

import concourse.bass as bass
from concourse import mybir
import numpy as np

F32 = mybir.dt.float32
F16 = mybir.dt.float16
U32 = mybir.dt.uint32
ALU = mybir.AluOpType
ACT = mybir.ActivationFunctionType
AX_X = mybir.AxisListType.X

P = 128
B, T, DIM = 4, 512, 128
H, KV, HD, NODES = 16, 4, 64, 4
TB = T // P
HP = H + 1
PAIRS = H // 2
HALF = HD // 2
E, HID = 8, 512
RW = 258
QKV = (H + 2 * KV) * HD
K0, V0 = H * HD, (H + KV) * HD
BIG = 32768.0
MAGIC = 12582912.0
TWO_PI_HI = 6.28125
TWO_PI_LO = 0.0019353071795864769
PI_CLAMP = 3.1415925
EPS = 1e-5
HEAD_T = 4
PTS_PER_B = 4 * H + 2


def block_kernel(nc, x, wq, wk, wv, wr, wo, w_router, w_up, w_gate, w_down, ws_up, ws_gate, ws_down,
                 c, wmod, inv_freq, out):
    ctx = ExitStack()
    with ctx:
        def sb(name, shape, dt=F32):
            return ctx.enter_context(nc.sbuf_tensor(name, shape, dt))

        def sem(name):
            return ctx.enter_context(nc.semaphore(name))

        ctx.enter_context(nc.allow_non_contiguous_dma(reason="small transposed loads"))
        psum = ctx.enter_context(nc.psum_tensor("psum", [P, 8, 512], F32))
        bank = [psum[:, i, :] for i in range(8)]
        psS = bank[0:4]
        psT12, psT3, psPT, psY = bank[4], bank[5], bank[6], bank[7]
        t12 = psT12[:, :].bitcast(F16)
        t3 = psT3[:, :].bitcast(F16)[:, 0:512]

        ident = sb("ident", [P, P])
        ident16 = sb("ident16", [P, P], F16)
        identbig = sb("identbig", [P, P], F16)
        causal = sb("causal", [P, P], F16)
        before = sb("before", [P, P], F16)
        ones16 = sb("ones16", [P, P], F16)
        bigrow = sb("bigrow", [P, P], F16)
        ones8 = sb("ones8", [E, P])
        half_pi = sb("half_pi", [P, 1])
        freq = sb("freq", [P, HALF])
        rank8 = sb("rank8", [P, E])

        w_qkv = sb("w_qkv", [P, QKV])
        w_r = sb("w_r", [P, H * NODES])
        w_o = sb("w_o", [P, PAIRS, DIM])
        w_rt = sb("w_rt", [P, E])

        c_t = sb("c_t", [P, B])
        c_e = sb("c_e", [P, B])
        c_s = sb("c_s", [P, B])
        mod = sb("mod", [P, 6, B])
        gsign = sb("gsign", [P, 2, B])
        gmag = sb("gmag", [P, 2, B])

        xb = sb("xb", [P, TB, DIM])
        stats = sb("stats", [P, TB, 6])
        mv = sb("mv", [P, TB, 2])
        ve = sb("ve", [P, TB])
        sd = sb("sd", [P, TB])
        rs = sb("rs", [P, 3, TB])
        xn = sb("xn", [P, TB, DIM])
        hT = sb("hT", [P, T])
        qkv = sb("qkv", [P, TB, QKV])
        lg = sb("lg", [P, TB, H, NODES])
        lmax = sb("lmax", [P, 2, TB * H])
        ew = sb("ew", [P, TB, H, NODES])
        member = sb("member", [P, TB, H, NODES])
        member16 = sb("member16", [P, TB, H, NODES], F16)
        wgt = sb("wgt", [P, TB, H, NODES])
        kmask = sb("kmask", [P, TB, HP, NODES], F16)
        is_a = sb("is_a", [P, TB, HP, NODES])
        pos = sb("pos", [P, TB, H, NODES])
        posn = sb("posn", [P, TB, H, NODES])
        slot = sb("slot", [P, TB, H, 2])
        cosn = sb("cosn", [P, TB, HP, 2, HALF])
        sinn = sb("sinn", [P, TB, HP, 2, HALF])

        pc = [sb(f"pc{s}", [P, TB, 2, HD]) for s in range(2)]
        ps = [sb(f"ps{s}", [P, TB, 2, HD]) for s in range(2)]
        gt, sc = [ps[i][:, :, :, :].rearrange("p t j d -> p (t j d)")[:, 0:6 * TB * H].rearrange(
            "p (k a) -> p k a", k=6) for i in range(2)]
        rot = pc
        pick = sb("pick", [P, 2, TB], U32)
        qk_all = sb("qk_all", [P, 2, NODES, 2, T], F16)
        kl_node = sb("kl_node", [P, 2 * NODES * T + NODES * TB * RW], F16)
        kl_all = kl_node[:, 0:2 * NODES * T].rearrange("p (u n t) -> p u n t", u=2, n=NODES)
        node = kl_node[:, 2 * NODES * T:].rearrange("p (n t c) -> p n t c", n=NODES, t=TB)
        qk_t = [[qk_all[:, u, n, :, :] for n in range(NODES)] for u in range(2)]
        kl_t = [[kl_all[0:HD + 1, u, n, :] for n in range(NODES)] for u in range(2)]
        NA = TB * H * 2
        ang = qk_all[:, :, :, :, :].rearrange("p u n a t -> p (u n a t)").bitcast(F32
              ).rearrange("p (a f) -> p a f", f=HALF)
        red = kl_node[:, 0:NA * HALF * 2].bitcast(F32).rearrange("p (a f) -> p a f", f=HALF)

        negmax = [sb(f"negmax{g}", [P, 2]) for g in range(2)]
        probs = [sb(f"probs{g}", [P, 2, T]) for g in range(2)]
        den = [sb(f"den{g}", [P, 2]) for g in range(2)]
        rden = [sb(f"rden{g}", [P, 2]) for g in range(2)]
        coef = [sb(f"coef{g}", [P, 2]) for g in range(2)]
        acc_all = sb("acc_all", [P, 2, 10 * P])
        acc = [[acc_all[:, u, ib * (ib + 1) // 2 * P:(ib + 1) * (ib + 2) // 2 * P] for ib in range(TB)]
               for u in range(2)]
        accT = [sb(f"accT{u}", [P, TB, T]) for u in range(2)]
        v_b = sb("v_b", [P, TB, HD])
        yT = sb("yT", [P, PAIRS + 1, T])

        x1 = sb("x1", [P, B * TB, DIM])
        h2T = sb("h2T", [P, B * T])
        rl = sb("rl", [P, TB, E])
        rr = sb("rr", [P, 4, TB, E])
        rm = sb("rm", [P, 4, TB])
        ecoef = sb("ecoef", [P, B * TB, E])
        att = xn[:, :, :].rearrange("p t d -> p (t d)")
        w_mod = probs[0][:, :, :].rearrange("p e t -> p (e t)")[:, 0:6 * DIM]
        w_e = [qkv[:, i, :].rearrange("p (k n) -> p k n", k=3) for i in range(2)]
        cos_flat = cosn[:, :, :, :, :].rearrange("p t h s f -> p (t h s f)")
        sin_flat = sinn[:, :, :, :, :].rearrange("p t h s f -> p (t h s f)")
        ffnT = cos_flat[:, 0:B * T]
        crow = cos_flat[0:E, B * T:2 * B * T]
        coefT = sin_flat[0:E, 0:B * T]
        hidden = [sin_flat[:, 2048 + 512 * i:2560 + 512 * i] for i in range(2)]
        gateb = [sin_flat[:, 3072 + 512 * i:3584 + 512 * i] for i in range(2)]
        bc = [ps[i][:, :, :, :].rearrange("p t j d -> p (t j d)") for i in range(2)]
        wtd = [pc[i][:, :, :, :].rearrange("p t j d -> p (t j d)") for i in range(2)]

        names = """loaded x_in w_in w_slot0 w_slot1 out_done const_done ident_done init_done
            c_exp c_sum c_rec c_silu mod_mm mod_raw mod_one mod_sign mod_mag mod_done
            bn_s bn_a var_e std_dev rs_0 rs_1 rs_2 rs_3 xn_done xn_t h_ready proj_mm q_ev kv_ev
            rank_g rank_s rank_m l_max l_sub l_exp l_mem l_sum l_rec w_done mem16 pos_mm pos_ev slots_w
            ang_mul ang_k ang_n ang_r1 ang_r2 ang_clamp ang_abs trig_sin trig_cos
            pc_done ps_done rot_done hi_done lo_done base_done pick_done node_done
            t_done t_ev scores_done negmax_done exp_done rden_done coef_done acc_done
            pt_done pt_ev pv_done y_ev vb_done
            wo_mm att_ev att_t x1_done x1_kept passed r_mm r_ev r_max r_sub r_exp r_eq r_rk r_rm r_sum r_rec r_c r_cT r_cTev r_cev
            h2_ev h2_copy crow_done bc_mm bc_ev gu_mm silu_done hid_done down_mm wtd_done ffn_acc hid_used
            fin_g fin_t fin_done""".split()
        S = {n: sem(n) for n in names}

        kv_of = lambda h: K0 + (h // (H // KV)) * HD

        def step_no(b, h, s):
            return b * (8 * H) + h * 8 + s

        def rot_no(b, h):
            return b * HP + h

        def pt_no(b, h, ib):
            return b * PTS_PER_B + 2 + h * 4 + ib

        def parts(s):
            v = node[:, 3 * s, :, 0:256].rearrange("p t (j c) -> p t j c", j=2)
            return v[:, :, :, 0:HD], v[:, :, :, HD:2 * HD]

        block = ctx.enter_context(nc.Block())

        @block.sync
        def _(sp):
            n_small = 0
            for dst, src in ((freq[:, :], inv_freq), (c_t[:, :], c.rearrange("b d -> d b")),
                             (w_mod[:, :], wmod), (w_qkv[:, 0:K0], wq), (w_qkv[:, K0:V0], wk),
                             (w_qkv[:, V0:QKV], wv), (w_r[:, :], wr),
                             (w_o[:, :, :], wo.rearrange("(c p) n -> p c n", p=P)), (w_rt[:, :], w_router)):
                sp.dma_start(dst, src).then_inc(S["loaded"], 16)
                n_small += 1
            with sp.Fori(0, B) as b:
                sp.wait_ge(S["x1_kept"], 1 + b)
                sp.dma_start(xb[:, :, :], x[bass.ds(b, 1), :, :].rearrange("a (t p) d -> p (a t) d", p=P)
                             ).then_inc(S["x_in"], 16)

        def load_expert(eng, i, up, gate, down):
            eng.dma_start(w_e[i][:, 0, :], up).then_inc(S[f"w_slot{i}"], 16)
            eng.dma_start(w_e[i][:, 1, :], gate).then_inc(S[f"w_slot{i}"], 16)
            eng.dma_start(w_e[i][:, 2, :].rearrange("p (c n) -> p c n", c=4),
                          down.rearrange("(c p) n -> p c n", p=P)).then_inc(S[f"w_slot{i}"], 16)

        @block.sync
        def _(sp):
            sp.wait_ge(S["wo_mm"], B)
            load_expert(sp, 0, ws_up, ws_gate, ws_down)
            load_expert(sp, 1, w_up[0], w_gate[0], w_down[0])
            with sp.Fori(0, 3) as r:
                for i in range(2):
                    e = r * 2 + 1 + i
                    sp.wait_ge(S["down_mm"], (r * 2 + 1 + i) * 4)
                    load_expert(sp, i, w_up[bass.ds(e, 1)].rearrange("a p n -> (a p) n"),
                                w_gate[bass.ds(e, 1)].rearrange("a p n -> (a p) n"),
                                w_down[bass.ds(e, 1)].rearrange("a p n -> (a p) n"))
            for b in range(B):
                sp.wait_ge(S["fin_done"], b + 1)
                sp.dma_start(out[b].rearrange("(t p) d -> p t d", p=P),
                             x1[:, b * TB:(b + 1) * TB, :]).then_inc(S["out_done"], 16)
            sp.wait_ge(S["out_done"], 16 * B)

        @block.gpsimd
        def _(pool):
            for t_, v in ((ident, 0.0), (ident16, 0.0), (identbig, 0.0), (causal, 0.0), (before, 1.0),
                          (ones16, 1.0), (bigrow, BIG), (ones8, 1.0), (half_pi, float(np.pi / 2))):
                pool.memset(t_[:, :], v).then_inc(S["const_done"], 1)
            pool.iota(rank8[:, :], [[-1, E]], base=E, channel_multiplier=0,
                      allow_small_or_imprecise_dtypes=True).then_inc(S["const_done"], 1)
            for u in range(2):
                pool.memset(acc_all[:, u, :], 0.0).then_inc(S["init_done"], 1)
                pool.memset(accT[u][:, :, :], 0.0).then_inc(S["init_done"], 1)
            pool.memset(v_b[:, :, :], 0.0).then_inc(S["init_done"], 1)
            pool.memset(cosn[:, :, H, :, :], 0.0).then_inc(S["init_done"], 1)
            pool.memset(sinn[:, :, H, :, :], 0.0).then_inc(S["init_done"], 1)
            pool.memset(kmask[:, :, H, :], 0.0).then_inc(S["init_done"], 1)
            pool.memset(is_a[:, :, H, :], 0.0).then_inc(S["init_done"], 1)
            pool.wait_ge(S["const_done"], 10)
            for t_, v in ((ident, 1.0), (ident16, 1.0), (identbig, BIG)):
                pool.affine_select(out=t_[:, :], in_=t_[:, :], compare_op=ALU.not_equal, fill=v, base=0,
                                   pattern=[[-1, P]], channel_multiplier=1).then_inc(S["ident_done"], 1)
            pool.affine_select(out=causal[:, :], in_=causal[:, :], compare_op=ALU.is_ge, fill=-BIG, base=0,
                               pattern=[[-1, P]], channel_multiplier=1).then_inc(S["ident_done"], 1)
            pool.affine_select(out=before[:, :], in_=before[:, :], compare_op=ALU.is_gt, fill=0.0, base=0,
                               pattern=[[1, P]], channel_multiplier=-1).then_inc(S["ident_done"], 1)

            pool.sem_inc(S["lo_done"], 1)

            def half_views(s, j):
                return [v[s][:, :, j, :].rearrange("p t (a f) -> p t a f", a=2) for v in (pc, ps)]

            def rotate_head(b, h):
                r = rot_no(b, h)
                pool.wait_ge(S["trig_cos"], b + 1)
                pool.wait_ge(S["q_ev"], (b + 1) * 8)
                pool.wait_ge(S["kv_ev"], (b + 1) * 4)
                pool.wait_ge(S["hi_done"], 1 + r * 2)
                pool.wait_ge(S["lo_done"], 1 + r * 2)
                for s in range(2):
                    cs, sn = [v[:, :, bass.ds(h, 1), s, :] for v in (cosn, sinn)]
                    for j, col in ((0, h * HD), (1, kv_of(h))):
                        src = qkv[:, :, bass.ds(col, HD)].rearrange("p t (a f) -> p t a f", a=2)
                        pool.tensor_tensor(half_views(s, j)[0], src, cs.to_broadcast([P, TB, 2, HALF]), ALU.mult
                                           ).then_inc(S["pc_done"], 1)
                        for half in range(2):
                            pool.tensor_tensor(ps[s][:, :, j, half * HALF:(half + 1) * HALF],
                                               qkv[:, :, bass.ds(col + (1 - half) * HALF, HALF)],
                                               sn.rearrange("p t a f -> p t (a f)"), ALU.mult
                                               ).then_inc(S["ps_done"], 1)
                for s in range(2):
                    pool.wait_ge(S["pc_done"], r * 4 + s * 2 + 2)
                    pool.wait_ge(S["ps_done"], r * 8 + s * 4 + 4)
                    for half, op in ((0, ALU.subtract), (1, ALU.add)):
                        sl = slice(half * HALF, (half + 1) * HALF)
                        pool.tensor_tensor(rot[s][:, :, :, sl], pc[s][:, :, :, sl], ps[s][:, :, :, sl], op
                                           ).then_inc(S["rot_done"], 1)
                pool.wait_ge(S["rot_done"], r * 4 + 4)
                for s in range(2):
                    pool.wait_ge(S["hi_done"], 1 + r * 2 + s + 1)
                    hi, lo = parts(s)
                    pool.tensor_tensor(lo, rot[s][:, :, :, :], hi, ALU.subtract).then_inc(S["lo_done"], 1)

            with pool.Fori(0, B) as b:
                with pool.Fori(0, HP) as h:
                    rotate_head(b, h)

        @block.scalar
        def _(act):
            act.wait_ge(S["loaded"], 16 * 9)
            act.activation(c_e[:, :], c_t[:, :], ACT.Exp, scale=-1.0).then_inc(S["c_exp"], 1)
            act.sem_inc(S["exp_done"], 3)
            for name in ("t_ev", "pt_ev", "y_ev", "vb_done"):
                act.sem_inc(S[name], 1)

            def norm_and_project(b, turn, which):
                act.wait_ge(S["var_e"], turn + 1)
                act.activation(sd[:, :], ve[:, :], ACT.Sqrt).then_inc(S["std_dev"], 1)
                act.wait_ge(S["xn_t"], turn + 1)
                act.wait_ge(S["mod_done"], 3)
                act.activation(hT[:, :], psPT[:, :], ACT.Identity,
                               bias=mod[:, which, bass.ds(b, 1)], scale=mod[:, which + 1, bass.ds(b, 1)]
                               ).then_inc(S["h_ready"], 1)

            def base(b, h):
                act.wait_ge(S["lo_done"], 1 + rot_no(b, h) * 2 + 2)
                nd = node[:, :, :, 0:256].bitcast(F32)
                for n in (1, 2):
                    act.activation(nd[:, n, :, :], nd[:, 3, :, :], ACT.Copy).then_inc(S["base_done"], 1)

            def move_pt(b, h, u, ib):
                j = pt_no(b, h, ib)
                act.wait_ge(S["pt_done"], 6 + j + 1)
                w = ib + 1
                act.activation(accT[u][:, 0:w, ib * P:(ib + 1) * P],
                               psPT[:, 0:w * P].rearrange("p (j i) -> p j i", j=w), ACT.Copy
                               ).then_inc(S["pt_ev"], 1)

            def evacuate_node(b, h, u, n):
                t = rot_no(b, h) * HEAD_T + n
                act.wait_ge(S["t_done"], 5 + t + 1)
                act.activation(qk_t[u][n].rearrange("p a t -> p (a t)"), t12, ACT.Copy
                               ).then_inc(S["t_ev"], 1)
                act.activation(kl_t[u][n], t3[0:HD + 1, :], ACT.Copy).then_inc(S["t_ev"], 1)

            with act.Fori(0, B) as b:
                norm_and_project(b, b * 2, 0)
                for tb in range(TB):
                    act.wait_ge(S["proj_mm"], b * TB + tb + 1)
                    for j in range(2):
                        act.activation(qkv[:, tb, j * 512:(j + 1) * 512], bank[4 * (tb % 2) + j][:, :], ACT.Copy,
                                       scale=HD ** -0.5).then_inc(S["q_ev"], 1)
                act.wait_ge(S["l_sub"], b + 1)
                act.activation(ew[:, :, :, :], ew[:, :, :, :], ACT.Exp).then_inc(S["l_exp"], 1)
                act.wait_ge(S["ang_clamp"], b + 1)
                act.activation(sinn[:, :, 0:H, :, :].rearrange("p t h s f -> p t (h s f)"),
                               red[:, :, :].rearrange("p (t a) f -> p t (a f)", t=TB), ACT.Sin
                               ).then_inc(S["trig_sin"], 1)
                act.activation(ang, ang, ACT.Abs).then_inc(S["ang_abs"], 1)
                act.wait_ge(S["ang_abs"], b + 1)
                act.activation(cosn[:, :, 0:H, :, :].rearrange("p t h s f -> p t (h s f)"),
                               ang[:, :, :].rearrange("p (t a) f -> p t (a f)", t=TB), ACT.Sin,
                               scale=-1.0, bias=half_pi[:, 0:1]).then_inc(S["trig_cos"], 1)
                base(b, 0)
                for n in range(NODES):
                    evacuate_node(b, 0, 0, n)
                with act.Fori(0, PAIRS) as hp:
                    for u in range(2):
                        h = hp * 2 + u
                        for s in range(8):
                            w = (s % 4 + 1) * P
                            g = s % 2
                            k = step_no(b, h, s)
                            act.wait_ge(S["negmax_done"], k + 1)
                            act.wait_ge(S["acc_done"], 1 + k * 2)
                            for e in range(2):
                                act.activation(probs[g][:, e, 0:w], psS[2 * g + e][:, 0:w], ACT.Exp,
                                               bias=negmax[g][:, e:e + 1], accum_out=den[g][:, e:e + 1]
                                               ).then_inc(S["exp_done"], 1)
                            if u == 0 and s == 1:
                                move_pt(b, h - 1, 1, 2)
                                move_pt(b, h - 1, 1, 3)
                                act.wait_ge(S["pv_done"], b * (PAIRS + 1) + hp + 1)
                                act.activation(yT[:, bass.ds(hp, 1), :].rearrange("p a t -> p (a t)"),
                                               psY[:, :], ACT.Copy).then_inc(S["y_ev"], 1)
                                act.activation(v_b[:, :, :], qkv[:, :, bass.ds((hp // 2) * HD + V0, HD)],
                                               ACT.Copy).then_inc(S["vb_done"], 1)
                            if u == 1 and s < 2:
                                move_pt(b, h - 1, 0, 2 + s)
                            if s == 2:
                                base(b, h + 1)
                            if s >= 4:
                                evacuate_node(b, h + 1, 1 - u, s - 4)
                            if s >= 6:
                                move_pt(b, h, u, s - 6)
                move_pt(b, H - 1, 1, 2)
                move_pt(b, H - 1, 1, 3)
                act.wait_ge(S["pv_done"], (b + 1) * (PAIRS + 1))
                act.activation(yT[:, PAIRS, :], psY[:, :], ACT.Copy).then_inc(S["y_ev"], 1)
                act.wait_ge(S["wo_mm"], b + 1)
                act.activation(att[:, :], psPT[:, :], ACT.Copy, scale=mod[:, 2, bass.ds(b, 1)]
                               ).then_inc(S["att_ev"], 1)
                norm_and_project(b, b * 2 + 1, 3)
                act.wait_ge(S["h_ready"], b * 2 + 2)
                act.activation(h2T[:, bass.ds(b * T, T)], hT[:, :], ACT.Copy).then_inc(S["h2_copy"], 1)
                act.wait_ge(S["r_sub"], b + 1)
                act.activation(rr[:, 0, :, :], rr[:, 0, :, :], ACT.Exp).then_inc(S["r_exp"], 1)

            def gates(n0):
                for i in range(16):
                    n = n0 + i
                    act.wait_ge(S["gu_mm"], n + 1)
                    act.wait_ge(S["hid_done"], n)
                    act.activation(gateb[i % 2][:, :], bank[i % 2][:, :], ACT.Silu).then_inc(S["silu_done"], 1)

            gates(0)
            gates(16)
            with act.Fori(0, 3) as r:
                gates(r * 32 + 32)
                gates(r * 32 + 48)
            for b in range(B):
                act.wait_ge(S["ffn_acc"], 32)
                act.activation(ffnT[:, b * T:(b + 1) * T], ffnT[:, b * T:(b + 1) * T], ACT.Copy,
                               scale=mod[:, 5, b:b + 1]).then_inc(S["fin_g"], 1)

        @block.vector
        def _(dve):
            dve.wait_ge(S["c_exp"], 1)
            dve.tensor_scalar(c_e[:, :], c_e[:, :], 1.0, None, ALU.add).then_inc(S["c_sum"], 1)
            dve.wait_ge(S["c_sum"], 1)
            dve.reciprocal(c_s[:, :], c_e[:, :]).then_inc(S["c_rec"], 1)
            dve.wait_ge(S["c_rec"], 1)
            dve.tensor_tensor(c_s[:, :], c_s[:, :], c_t[:, :], ALU.mult).then_inc(S["c_silu"], 1)
            dve.wait_ge(S["mod_mm"], 1)
            dve.tensor_copy(mod[:, :, :].rearrange("p a b -> p (a b)"), psT12[:, 0:6 * B]).then_inc(S["mod_raw"], 1)
            dve.wait_ge(S["mod_raw"], 1)
            for j in range(2):
                dve.tensor_scalar(mod[:, 3 * j + 1, :], mod[:, 3 * j + 1, :], 1.0, None, ALU.add
                                  ).then_inc(S["mod_done"], 1)
            g_raw = mod[:, :, :].rearrange("p (j k) b -> p j k b", j=2)[:, :, 2, :]
            dve.tensor_scalar(gsign[:, :, :], g_raw, 0.0, 2.0, ALU.is_ge, ALU.mult).then_inc(S["mod_sign"], 1)
            dve.scalar_tensor_tensor(gmag[:, :, :], g_raw, -1.0, g_raw, ALU.mult, ALU.max).then_inc(S["mod_sign"], 1)
            dve.wait_ge(S["mod_sign"], 2)
            dve.tensor_scalar(gmag[:, :, :], gmag[:, :, :], 0.25, None, ALU.max).then_inc(S["mod_mag"], 1)
            dve.wait_ge(S["mod_mag"], 1)
            dve.scalar_tensor_tensor(g_raw, gsign[:, :, :], -1.0, gmag[:, :, :], ALU.add, ALU.mult
                                     ).then_inc(S["mod_done"], 1)

            def layer_norm(turn):
                for tb in range(TB):
                    dve.bn_stats(stats[:, tb, :], xb[:, tb, :]).then_inc(S["bn_s"], 1)
                dve.wait_ge(S["bn_s"], (turn + 1) * TB)
                dve.sem_inc(S["passed"], 1)
                for tb in range(TB):
                    dve.bn_aggr(mv[:, tb, :], stats[:, tb, :]).then_inc(S["bn_a"], 1)
                dve.wait_ge(S["bn_a"], (turn + 1) * TB)
                dve.tensor_scalar(ve[:, :], mv[:, :, 1], EPS, None, ALU.add).then_inc(S["var_e"], 1)
                dve.wait_ge(S["std_dev"], turn + 1)
                dve.reciprocal(rs[:, 0, :], sd[:, :]).then_inc(S["rs_0"], 1)
                dve.wait_ge(S["rs_0"], turn + 1)
                dve.tensor_tensor(rs[:, 1, :], rs[:, 0, :], rs[:, 0, :], ALU.mult).then_inc(S["rs_1"], 1)
                dve.wait_ge(S["rs_1"], turn + 1)
                dve.scalar_tensor_tensor(rs[:, 2, :], rs[:, 1, :], -0.5, ve[:, :], ALU.mult, ALU.mult
                                         ).then_inc(S["rs_2"], 1)
                dve.wait_ge(S["rs_2"], turn + 1)
                dve.scalar_tensor_tensor(rs[:, 1, :], rs[:, 2, :], 1.5, rs[:, 0, :], ALU.add, ALU.mult
                                         ).then_inc(S["rs_3"], 1)
                dve.wait_ge(S["rs_3"], turn + 1)
                for tb in range(TB):
                    dve.tensor_scalar(xn[:, tb, :], xb[:, tb, :], mv[:, tb, 0:1], rs[:, 1, tb:tb + 1],
                                      ALU.subtract, ALU.mult).then_inc(S["xn_done"], 1)

            def high(b, h):
                r = rot_no(b, h)
                dve.wait_ge(S["rot_done"], r * 4 + 4)
                dve.wait_ge(S["t_done"], 1 + r * 4)
                for s in range(2):
                    dve.tensor_copy(parts(s)[0], rot[s][:, :, :, :]).then_inc(S["hi_done"], 1)

            def masks(b, h):
                r = rot_no(b, h)
                dve.tensor_copy(pick[:, :, :].rearrange("p n t -> p t n"),
                                is_a[:, :, bass.ds(h, 1), 1:3].rearrange("p t a n -> p t (a n)")
                                ).then_inc(S["pick_done"], 1)
                dve.tensor_copy(node[:, :, :, 256].rearrange("p n t -> p t n"),
                                kmask[:, :, bass.ds(h, 1), :].rearrange("p t a n -> p t (a n)")
                                ).then_inc(S["pick_done"], 1)

            def choose(b, h):
                r = rot_no(b, h)
                dve.wait_ge(S["base_done"], r * 2 + 2)
                dve.wait_ge(S["pick_done"], r * 2 + 2)
                dve.sem_inc(S["passed"], 1)
                nd = node[:, :, :, 0:256].bitcast(U32)
                for n in (1, 2):
                    dve.copy_predicated(nd[:, n, :, :], pick[:, n - 1, :].unsqueeze(2).to_broadcast([P, TB, 128]),
                                        nd[:, 0, :, :]).then_inc(S["node_done"], 1)

            def inverse_sums(b, h, s):
                k = step_no(b, h, s)
                dve.wait_ge(S["exp_done"], 3 + k * 2 + 2)
                dve.reciprocal(rden[s % 2][:, :], den[s % 2][:, :]).then_inc(S["rden_done"], 1)

            def weigh(b, h, u, s):
                k = step_no(b, h, s)
                g, ib, n0 = s % 2, s % 4, 2 * (s // 4)
                w = (ib + 1) * P
                dve.wait_ge(S["rden_done"], k + 1)
                dve.tensor_tensor(coef[g][:, :], rden[g][:, :],
                                  wgt[:, ib, bass.ds(h, 1), n0:n0 + 2].rearrange("p a n -> p (a n)"), ALU.mult
                                  ).then_inc(S["coef_done"], 1)
                dve.wait_ge(S["coef_done"], k + 1)
                if s < 4:
                    dve.wait_ge(S["pt_done"], 1 + b * PTS_PER_B + h * 4 + ib)
                    dve.tensor_scalar(acc[u][ib], probs[g][:, 0, 0:w], coef[g][:, 0:1], None, ALU.mult
                                      ).then_inc(S["acc_done"], 1)
                else:
                    dve.wait_ge(S["acc_done"], 3 + (k - 4) * 2 + 2)
                    dve.scalar_tensor_tensor(acc[u][ib], probs[g][:, 0, 0:w], coef[g][:, 0:1], acc[u][ib],
                                             ALU.mult, ALU.add).then_inc(S["acc_done"], 1)
                dve.wait_ge(S["acc_done"], 3 + k * 2 + 1)
                dve.scalar_tensor_tensor(acc[u][ib], probs[g][:, 1, 0:w], coef[g][:, 1:2], acc[u][ib],
                                         ALU.mult, ALU.add).then_inc(S["acc_done"], 1)

            dve.sem_inc(S["acc_done"], 3)
            dve.sem_inc(S["hi_done"], 1)
            dve.sem_inc(S["x1_kept"], 1)
            dve.wait_ge(S["ident_done"], 5)
            dve.wait_ge(S["init_done"], 9)
            with dve.Fori(0, B) as b:
                dve.wait_ge(S["x_in"], (b + 1) * 16)
                layer_norm(b * 2)
                for tb in range(TB):
                    dve.wait_ge(S["proj_mm"], b * TB + tb + 1)
                    o = 4 * (tb % 2)
                    dve.tensor_copy(qkv[:, tb, K0:QKV], bank[o + 2][:, :]).then_inc(S["kv_ev"], 1)
                    dve.tensor_copy(lg[:, tb, :, :].rearrange("p h n -> p (h n)"),
                                    bank[o + 3][:, 0:H * NODES]).then_inc(S["rank_g"], 1)
                dve.wait_ge(S["rank_g"], (b + 1) * TB)
                L = lg[:, :, :, :].rearrange("p t h n -> p (t h) n")
                M = member[:, :, :, :].rearrange("p t h n -> p (t h) n")
                W = ew[:, :, :, :].rearrange("p t h n -> p (t h) n")
                duo = [(0, 1), (0, 2), (0, 3), (1, 2), (1, 3), (2, 3)]
                for i, (m, n) in enumerate(duo):
                    dve.tensor_tensor(gt[:, i, :], L[:, :, m], L[:, :, n], ALU.is_ge).then_inc(S["rank_s"], 1)
                dve.tensor_reduce(lmax[:, 0, :], L, AX_X, ALU.max).then_inc(S["l_max"], 1)
                dve.wait_ge(S["l_max"], b + 1)
                dve.tensor_tensor(W, L, lmax[:, 0, :].unsqueeze(2).to_broadcast([P, TB * H, NODES]), ALU.subtract
                                  ).then_inc(S["l_sub"], 1)
                dve.wait_ge(S["rank_s"], (b + 1) * 6)
                for i, (a, c_, op) in enumerate(((0, 1, ALU.add), (3, 4, ALU.add), (5, 1, ALU.subtract),
                                                 (2, 4, ALU.add))):
                    dve.tensor_tensor(sc[:, i, :], gt[:, a, :], gt[:, c_, :], op).then_inc(S["rank_m"], 1)
                dve.wait_ge(S["rank_m"], b * 8 + 4)
                for i, a, op in ((0, 2, ALU.add), (1, 0, ALU.subtract), (2, 3, ALU.subtract), (3, 5, ALU.add)):
                    dve.tensor_tensor(sc[:, i, :], sc[:, i, :], gt[:, a, :], op).then_inc(S["rank_m"], 1)
                dve.wait_ge(S["rank_m"], b * 8 + 8)
                for n, (v, op) in enumerate(((1.5, ALU.is_gt), (0.5, ALU.is_gt), (-0.5, ALU.is_gt), (1.5, ALU.is_lt))):
                    dve.tensor_scalar(M[:, :, n], sc[:, n, :], v, None, op).then_inc(S["l_mem"], 1)
                dve.wait_ge(S["l_mem"], (b + 1) * 4)
                dve.tensor_copy(member16[:, :, :, :], member[:, :, :, :]).then_inc(S["mem16"], 1)
                dve.tensor_scalar(kmask[:, :, 0:H, :].rearrange("p t h n -> p t (h n)"),
                                  member[:, :, :, :].rearrange("p t h n -> p t (h n)"), 1.0, BIG,
                                  ALU.subtract, ALU.mult).then_inc(S["mem16"], 1)
                dve.wait_ge(S["l_exp"], b + 1)
                dve.tensor_tensor(wgt[:, :, :, :], ew[:, :, :, :], member[:, :, :, :], ALU.mult
                                  ).then_inc(S["l_sum"], 1)
                dve.wait_ge(S["l_sum"], b * 2 + 1)
                G = wgt[:, :, :, :].rearrange("p t h n -> p (t h) n")
                dve.tensor_reduce(lmax[:, 1, :], G, AX_X, ALU.add).then_inc(S["l_sum"], 1)
                dve.wait_ge(S["l_sum"], b * 2 + 2)
                dve.reciprocal(lmax[:, 0, :], lmax[:, 1, :]).then_inc(S["l_rec"], 1)
                dve.wait_ge(S["l_rec"], b + 1)
                dve.tensor_tensor(G, G, lmax[:, 0, :].unsqueeze(2).to_broadcast([P, TB * H, NODES]), ALU.mult
                                  ).then_inc(S["w_done"], 1)
                A = lambda n: is_a[:, :, 0:H, n]
                Mb = lambda n: member[:, :, :, n]
                dve.tensor_copy(A(0), Mb(0)).then_inc(S["slots_w"], 1)
                dve.tensor_tensor(A(1), Mb(1), Mb(0), ALU.is_gt).then_inc(S["slots_w"], 1)
                dve.tensor_tensor(A(2), Mb(2), Mb(3), ALU.mult).then_inc(S["slots_w"], 1)
                dve.memset(A(3), 0.0).then_inc(S["slots_w"], 1)
                dve.wait_ge(S["pos_mm"], b + 1)
                dve.tensor_copy(pos[:, :, :, :].rearrange("p t h n -> p (t h n)"), psPT[:, 0:TB * H * NODES]
                                ).then_inc(S["pos_ev"], 1)
                dve.wait_ge(S["pos_ev"], b + 1)
                dve.wait_ge(S["slots_w"], b * 9 + 4)
                dve.tensor_tensor(posn[:, :, :, :], pos[:, :, :, :], is_a[:, :, 0:H, :], ALU.mult
                                  ).then_inc(S["slots_w"], 1)
                dve.tensor_tensor(pos[:, :, :, :], pos[:, :, :, :], member[:, :, :, :], ALU.mult
                                  ).then_inc(S["slots_w"], 1)
                dve.wait_ge(S["slots_w"], b * 9 + 6)
                SL = slot[:, :, :, :].rearrange("p t h s -> p (t h) s")
                dve.tensor_reduce(SL[:, :, 0], posn[:, :, :, :].rearrange("p t h n -> p (t h) n"), AX_X, ALU.add
                                  ).then_inc(S["slots_w"], 1)
                dve.tensor_reduce(SL[:, :, 1], pos[:, :, :, :].rearrange("p t h n -> p (t h) n"), AX_X, ALU.add
                                  ).then_inc(S["slots_w"], 1)
                dve.wait_ge(S["slots_w"], b * 9 + 8)
                dve.tensor_tensor(SL[:, :, 1], SL[:, :, 1], SL[:, :, 0], ALU.subtract).then_inc(S["slots_w"], 1)
                dve.wait_ge(S["slots_w"], b * 9 + 9)
                sp_ = slot[:, :, :, :].rearrange("p t h s -> p (t h s)").unsqueeze(2).to_broadcast([P, NA, HALF])
                dve.tensor_tensor(ang[:, :, :], sp_, freq[:, :].unsqueeze(1).to_broadcast([P, NA, HALF]), ALU.mult
                                  ).then_inc(S["ang_mul"], 1)
                dve.wait_ge(S["ang_mul"], b + 1)
                dve.tensor_scalar(red[:, :, :], ang[:, :, :], float(1 / (2 * np.pi)), MAGIC, ALU.mult, ALU.add
                                  ).then_inc(S["ang_k"], 1)
                dve.wait_ge(S["ang_k"], b + 1)
                dve.tensor_scalar(red[:, :, :], red[:, :, :], MAGIC, None, ALU.subtract).then_inc(S["ang_n"], 1)
                dve.wait_ge(S["ang_n"], b + 1)
                dve.scalar_tensor_tensor(ang[:, :, :], red[:, :, :], -TWO_PI_HI, ang[:, :, :], ALU.mult, ALU.add
                                         ).then_inc(S["ang_r1"], 1)
                dve.wait_ge(S["ang_r1"], b + 1)
                dve.scalar_tensor_tensor(ang[:, :, :], red[:, :, :], -TWO_PI_LO, ang[:, :, :], ALU.mult, ALU.add
                                         ).then_inc(S["ang_r2"], 1)
                dve.wait_ge(S["ang_r2"], b + 1)
                dve.tensor_scalar(red[:, :, :], ang[:, :, :], PI_CLAMP, -PI_CLAMP, ALU.min, ALU.max
                                  ).then_inc(S["ang_clamp"], 1)
                high(b, 0)
                masks(b, 0)
                choose(b, 0)
                with dve.Fori(0, PAIRS) as hp:
                    for u in range(2):
                        h = hp * 2 + u
                        for s in range(8):
                            g, w = s % 2, (s % 4 + 1) * P
                            k = step_no(b, h, s)
                            if s:
                                inverse_sums(b, h, s - 1)
                            dve.wait_ge(S["scores_done"], k + 1)
                            dve.tensor_reduce(negmax[g][:, :], psum[:, 2 * g:2 * g + 2, 0:w], AX_X, ALU.max,
                                              negate=True).then_inc(S["negmax_done"], 1)
                            if s:
                                weigh(b, h, u, s - 1)
                            if s == 1:
                                high(b, h + 1)
                            if s == 2:
                                masks(b, h + 1)
                            if s == 3:
                                choose(b, h + 1)
                        inverse_sums(b, h, 7)
                        weigh(b, h, u, 7)
                dve.wait_ge(S["att_t"], b + 1)
                dve.tensor_tensor(xb[:, :, :], psY[:, :].rearrange("p (t d) -> p t d", t=TB), xb[:, :, :], ALU.add
                                  ).then_inc(S["x1_done"], 1)
                dve.wait_ge(S["x1_done"], b + 1)
                layer_norm(b * 2 + 1)
                dve.tensor_copy(x1[:, bass.ds(b * TB, TB), :], xb[:, :, :]).then_inc(S["x1_kept"], 1)
                dve.wait_ge(S["r_mm"], b + 1)
                dve.tensor_copy(rl[:, :, :].rearrange("p t e -> p (t e)"), psT12[:, 0:TB * E]).then_inc(S["r_ev"], 1)
                dve.wait_ge(S["r_ev"], b + 1)
                dve.tensor_reduce(rm[:, 0, :], rl[:, :, :], AX_X, ALU.max).then_inc(S["r_max"], 1)
                dve.wait_ge(S["r_max"], b + 1)
                top = rm[:, 0, :].unsqueeze(2).to_broadcast([P, TB, E])
                dve.tensor_tensor(rr[:, 0, :, :], rl[:, :, :], top, ALU.subtract).then_inc(S["r_sub"], 1)
                dve.tensor_tensor(rr[:, 1, :, :], rl[:, :, :], top, ALU.is_ge).then_inc(S["r_eq"], 1)
                dve.wait_ge(S["r_eq"], b + 1)
                dve.tensor_tensor(rr[:, 2, :, :], rr[:, 1, :, :], rank8[:, :].unsqueeze(1).to_broadcast([P, TB, E]),
                                  ALU.mult).then_inc(S["r_rk"], 1)
                dve.wait_ge(S["r_rk"], b + 1)
                dve.tensor_reduce(rm[:, 1, :], rr[:, 2, :, :], AX_X, ALU.max).then_inc(S["r_rm"], 1)
                dve.wait_ge(S["r_exp"], b + 1)
                dve.tensor_reduce(rm[:, 2, :], rr[:, 0, :, :], AX_X, ALU.add).then_inc(S["r_sum"], 1)
                dve.wait_ge(S["r_sum"], b + 1)
                dve.reciprocal(rm[:, 3, :], rm[:, 2, :]).then_inc(S["r_rec"], 1)
                dve.wait_ge(S["r_rm"], b + 1)
                dve.tensor_tensor(rr[:, 1, :, :], rr[:, 2, :, :], rm[:, 1, :].unsqueeze(2).to_broadcast([P, TB, E]),
                                  ALU.is_equal).then_inc(S["r_c"], 1)
                dve.wait_ge(S["r_c"], b * 2 + 1)
                dve.wait_ge(S["r_rec"], b + 1)
                dve.scalar_tensor_tensor(rr[:, 3, :, :], rr[:, 1, :, :], 2.0,
                                         rm[:, 3, :].unsqueeze(2).to_broadcast([P, TB, E]), ALU.mult, ALU.mult
                                         ).then_inc(S["r_c"], 1)
                dve.wait_ge(S["r_c"], b * 2 + 2)
                dve.tensor_copy(ecoef[:, bass.ds(b * TB, TB), :], rr[:, 3, :, :]).then_inc(S["r_cev"], 1)

            for t_ in range(B):
                dve.wait_ge(S["r_cT"], t_ + 1)
                dve.tensor_copy(coefT[:, t_ * T:(t_ + 1) * T], bank[4 + t_][0:E, :]).then_inc(S["r_cTev"], 1)
            dve.sem_inc(S["hid_done"], 1)

            def coef_row(m):
                dve.wait_ge(S["bc_mm"], (m - 1) * 4)
                dve.wait_ge(S["r_cTev"], B)
                dve.tensor_scalar(crow[:, :], coefT[:, :], ident[0:E, bass.ds(m - 1, 1)] if not isinstance(m, int)
                                  else ident[0:E, m - 1:m], None, ALU.mult).then_inc(S["crow_done"], 1)

            def hidden_and_sum(m, shared):
                n0 = m * 16
                if not shared:
                    coef_row(m)

                def total(t_):
                    o = t_ % 2
                    dst = ffnT[:, t_ * 512:(t_ + 1) * 512]
                    dve.wait_ge(S["down_mm"], m * 4 + t_ + 1)
                    if shared:
                        dve.tensor_copy(dst, bank[4 + o][:, :]).then_inc(S["ffn_acc"], 1)
                        return
                    dve.wait_ge(S["bc_mm"], (m - 1) * 4 + t_ + 1)
                    dve.tensor_copy(bc[o][:, :], bank[6 + o][:, :]).then_inc(S["bc_ev"], 1)
                    dve.wait_ge(S["bc_ev"], (m - 1) * 4 + t_ + 1)
                    dve.tensor_tensor(wtd[o][:, :], bank[4 + o][:, :], bc[o][:, :], ALU.mult
                                      ).then_inc(S["wtd_done"], 1)
                    dve.wait_ge(S["wtd_done"], (m - 1) * 4 + t_ + 1)
                    dve.wait_ge(S["ffn_acc"], m * 4 + t_ - 3)
                    dve.tensor_tensor(dst, dst, wtd[o][:, :], ALU.add).then_inc(S["ffn_acc"], 1)

                for t_ in range(B):
                    for c_ in range(4):
                        i = t_ * 4 + c_
                        dve.wait_ge(S["silu_done"], n0 + i + 1)
                        if not (shared and i < 2):
                            dve.wait_ge(S["hid_used"], n0 + i - 1)
                        dve.tensor_tensor(hidden[i % 2][:, :], bank[2 + i % 2][:, :], gateb[i % 2][:, :],
                                          ALU.mult).then_inc(S["hid_done"], 1)
                        if c_ == 1 and t_:
                            total(t_ - 1)
                total(3)

            hidden_and_sum(0, True)
            hidden_and_sum(1, False)
            with dve.Fori(0, 3) as r:
                hidden_and_sum(r * 2 + 2, False)
                hidden_and_sum(r * 2 + 3, False)
            for b in range(B):
                dve.wait_ge(S["fin_t"], b + 1)
                dve.tensor_tensor(x1[:, b * TB:(b + 1) * TB, :],
                                  bank[b % 2][:, :].rearrange("p (t d) -> p t d", t=TB),
                                  x1[:, b * TB:(b + 1) * TB, :], ALU.add).then_inc(S["fin_done"], 1)

        @block.tensor
        def _(pe):
            pe.wait_ge(S["c_silu"], 1)
            pe.wait_ge(S["loaded"], 16 * 9)
            for j in range(6):
                mm = pe.matmul(psT12[:, j * B:(j + 1) * B], w_mod[:, j * DIM:(j + 1) * DIM], c_s[:, :],
                               start=True, stop=True)
            mm.then_inc(S["mod_mm"], 1)
            pe.wait_ge(S["ident_done"], 5)
            pe.wait_ge(S["init_done"], 9)
            pe.sem_inc(S["t_done"], 5)
            pe.sem_inc(S["pt_done"], 6)

            def norm_rows(turn):
                pe.wait_ge(S["xn_done"], (turn + 1) * TB)
                for tb in range(TB):
                    mm = pe.transpose(psPT[:, tb * P:(tb + 1) * P], xn[:, tb, :], ident[:, :])
                mm.then_inc(S["xn_t"], 1)

            def node_tiles(b, h, u, n):
                t = rot_no(b, h) * HEAD_T + n
                pe.wait_ge(S["node_done"], rot_no(b, h) * 2 + 2)
                pe.wait_ge(S["t_ev"], 1 + t * 2)
                for tb in range(TB):
                    nd = node[:, n, tb, :]
                    pe.transpose(t12[:, tb * P:(tb + 1) * P], nd[:, 0:P], ident16[:, :])
                    for half in range(2):
                        pe.transpose(t12[half * HD:(half + 1) * HD, T + tb * P:T + (tb + 1) * P],
                                     nd[:, P:P + HD], ident16[:, :])
                for tb in range(TB):
                    mm = pe.transpose(t3[0:HD + 1, tb * P:(tb + 1) * P], node[:, n, tb, P + HD:P + 2 * HD + 1],
                                      ident16[:, :])
                mm.then_inc(S["t_done"], 1)

            def scores(b, h, u, s):
                k = step_no(b, h, s)
                g, ib, n0 = s % 2, s % 4, 2 * (s // 4)
                w = (ib + 1) * P
                if ib == 0:
                    t = rot_no(b, h) * HEAD_T + n0 + 2
                    pe.wait_ge(S["t_ev"], 1 + t * 2)
                pe.wait_ge(S["exp_done"], 1 + k * 2)
                rows = slice(ib * P, (ib + 1) * P)
                for e in range(2):
                    n, o = n0 + e, psS[2 * g + e]
                    pe.matmul(o[:, 0:w], qk_t[u][n][:, 0, rows], qk_t[u][n][:, 1, 0:w], start=True, stop=False)
                    pe.matmul(o[:, 0:w], qk_t[u][n][0:HD, 0, rows], kl_t[u][n][0:HD, 0:w], start=False, stop=False)
                    pe.matmul(o[:, 0:w], bigrow[HD:HD + 1, :], kl_t[u][n][HD:HD + 1, 0:w], start=False, stop=False)
                    mm = pe.matmul(o[:, ib * P:w], identbig[:, :], causal[:, :], start=False, stop=True)
                mm.then_inc(S["scores_done"], 1)

            def prob_rows(b, h, u, ib):
                j = pt_no(b, h, ib)
                pe.wait_ge(S["acc_done"], 3 + step_no(b, h, 4 + ib) * 2 + 2)
                pe.wait_ge(S["pt_ev"], 1 + j)
                for jb in range(ib + 1):
                    mm = pe.transpose(psPT[:, jb * P:(jb + 1) * P], acc[u][ib][:, jb * P:(jb + 1) * P], ident[:, :])
                mm.then_inc(S["pt_done"], 1)

            def values(b, hp):
                pe.wait_ge(S["pt_ev"], 1 + b * PTS_PER_B + hp * 8 + 2)
                pe.wait_ge(S["vb_done"], 1 + b * PAIRS + hp)
                pe.wait_ge(S["y_ev"], 1 + b * (PAIRS + 1) + hp)
                for jb in range(TB):
                    for u in range(2):
                        mm = pe.matmul(psY[u * HD:(u + 1) * HD, jb * P:T], v_b[:, jb, :], accT[u][:, jb, jb * P:T],
                                       start=(jb == 0), stop=(jb == TB - 1))
                mm.then_inc(S["pv_done"], 1)

            with pe.Fori(0, B) as b:
                norm_rows(b * 2)
                pe.wait_ge(S["h_ready"], b * 2 + 1)
                for tb in range(TB):
                    o = 4 * (tb % 2)
                    if tb >= 2:
                        pe.wait_ge(S["q_ev"], b * 8 + (tb - 1) * 2)
                        pe.wait_ge(S["rank_g"], b * TB + tb - 1)
                    lhs = hT[:, tb * P:(tb + 1) * P]
                    for j in range(3):
                        pe.matmul(bank[o + j][:, :], lhs, w_qkv[:, j * 512:(j + 1) * 512], start=True, stop=True)
                    pe.matmul(bank[o + 3][:, 0:H * NODES], lhs, w_r[:, :], start=True, stop=True
                              ).then_inc(S["proj_mm"], 1)
                pe.wait_ge(S["q_ev"], (b + 1) * 8)
                pe.wait_ge(S["mem16"], b * 2 + 1)
                for tb in range(TB):
                    dst = psPT[:, tb * 64:(tb + 1) * 64]
                    for sb_ in range(tb + 1):
                        mm = pe.matmul(dst, before[:, :] if sb_ == tb else ones16[:, :],
                                       member16[:, sb_, :, :].rearrange("p h n -> p (h n)"),
                                       start=(sb_ == 0), stop=(sb_ == tb))
                mm.then_inc(S["pos_mm"], 1)
                for n in range(NODES):
                    node_tiles(b, 0, 0, n)
                with pe.Fori(0, PAIRS) as hp:
                    for u in range(2):
                        h = hp * 2 + u
                        for s in range(8):
                            scores(b, h, u, s)
                            if u == 0 and s == 1:
                                prob_rows(b, h - 1, 1, 2)
                                prob_rows(b, h - 1, 1, 3)
                                values(b, hp)
                            if u == 1 and s < 2:
                                prob_rows(b, h - 1, 0, 2 + s)
                            if s >= 4:
                                node_tiles(b, h + 1, 1 - u, s - 4)
                            if s >= 6:
                                prob_rows(b, h, u, s - 6)
                prob_rows(b, H - 1, 1, 2)
                prob_rows(b, H - 1, 1, 3)
                values(b, PAIRS)
                pe.wait_ge(S["y_ev"], 1 + (b + 1) * (PAIRS + 1))
                for i in range(PAIRS):
                    mm = pe.matmul(psPT[:, :], w_o[:, i, :], yT[:, i + 1, :], start=(i == 0), stop=(i == PAIRS - 1))
                mm.then_inc(S["wo_mm"], 1)
                pe.wait_ge(S["att_ev"], b + 1)
                for tb in range(TB):
                    mm = pe.transpose(psY[:, tb * P:(tb + 1) * P], att[:, tb * P:(tb + 1) * P], ident[:, :])
                mm.then_inc(S["att_t"], 1)
                norm_rows(b * 2 + 1)
                pe.wait_ge(S["h_ready"], b * 2 + 2)
                for tb in range(TB):
                    mm = pe.matmul(psT12[:, tb * E:(tb + 1) * E], hT[:, tb * P:(tb + 1) * P], w_rt[:, :],
                                   start=True, stop=True)
                mm.then_inc(S["r_mm"], 1)
            pe.wait_ge(S["h2_copy"], B)
            pe.wait_ge(S["r_cev"], B)
            for t_ in range(B):
                for tb in range(TB):
                    mm = pe.transpose(bank[4 + t_][0:E, tb * P:(tb + 1) * P], ecoef[:, t_ * TB + tb, :], ident[:, :])
                mm.then_inc(S["r_cT"], 1)

            def ffn(m, slot_, shared, w_count):
                n0 = m * 16
                w = w_e[slot_]
                pe.wait_ge(S[f"w_slot{slot_}"], w_count)

                def gate_up(i):
                    t_, c_ = i // 4, i % 4
                    if not (shared and i < 2):
                        pe.wait_ge(S["silu_done"], n0 + i - 1)
                        pe.wait_ge(S["hid_done"], n0 + i)
                    rhs = h2T[:, t_ * 512:(t_ + 1) * 512]
                    pe.matmul(bank[i % 2][:, :], w[:, 1, c_ * P:(c_ + 1) * P], rhs, start=True, stop=True)
                    pe.matmul(bank[2 + i % 2][:, :], w[:, 0, c_ * P:(c_ + 1) * P], rhs, start=True, stop=True
                              ).then_inc(S["gu_mm"], 1)

                def down(i):
                    t_, c_ = i // 4, i % 4
                    o = t_ % 2
                    if c_ == 0:
                        if not (shared and t_ < 2):
                            pe.wait_ge(S["ffn_acc"], m * 4 + t_ - 1)
                        if not shared:
                            pe.wait_ge(S["crow_done"], m)
                            pe.matmul(bank[6 + o][:, :], ones8[:, :], crow[:, t_ * 512:(t_ + 1) * 512],
                                      start=True, stop=True).then_inc(S["bc_mm"], 1)
                    pe.wait_ge(S["hid_done"], n0 + i + 2)
                    mm = pe.matmul(bank[4 + o][:, :], w[:, 2, c_ * P:(c_ + 1) * P], hidden[i % 2][:, :],
                                   start=(c_ == 0), stop=(c_ == 3))
                    mm.then_inc(S["hid_used"], 1)
                    if c_ == 3:
                        pe.wait_ge(S["hid_used"], n0 + i + 1)
                        pe.sem_inc(S["down_mm"], 1)

                gate_up(0)
                for i in range(1, 17):
                    if i < 16:
                        gate_up(i)
                    down(i - 1)

            ffn(0, 0, True, 48)
            ffn(1, 1, False, 48)
            with pe.Fori(0, 3) as r:
                ffn(r * 2 + 2, 0, False, r * 48 + 96)
                ffn(r * 2 + 3, 1, False, r * 48 + 96)
            for b in range(B):
                pe.wait_ge(S["fin_g"], b + 1)
                if b >= 2:
                    pe.wait_ge(S["fin_done"], b - 1)
                for tb in range(TB):
                    mm = pe.transpose(bank[b % 2][:, tb * P:(tb + 1) * P],
                                      ffnT[:, b * T + tb * P:b * T + (tb + 1) * P], ident[:, :])
                mm.then_inc(S["fin_t"], 1)


_INS = ['L0_attn_x', 'L0_attn_wq', 'L0_attn_wk', 'L0_attn_wv', 'L0_attn_wr', 'L0_attn_wo', 'L0_ffn_w_router',
        'L0_ffn_w_up', 'L0_ffn_w_gate', 'L0_ffn_w_down', 'L0_ffn_ws_up', 'L0_ffn_ws_gate', 'L0_ffn_ws_down',
        'L0_c', 'L0_wmod']
_OUTS = [((B, T, DIM), 'float32')]


def _rotary_frequencies():
    e = np.arange(0, HD, 2, dtype=np.float32) / np.float32(HD)
    f = np.float32(1.0) / np.power(np.float32(10000.0), e, dtype=np.float32)
    return np.ascontiguousarray(np.broadcast_to(f.astype(np.float32), (P, HALF)))


def kernel(**inputs):
    import numpy as _np
    import concourse.bacc as _bacc
    from concourse import mybir as _mybir
    from concourse.bass_utils import run_bass_kernel_spmd as _run

    nc = _bacc.Bacc("TRN2", target_bir_lowering=False, num_devices=1)
    arrays, args = {}, []
    for name in _INS:
        a = _np.ascontiguousarray(inputs[name])
        arrays[f"in_{name}_dram"] = a
        args.append(nc.dram_tensor(f"in_{name}_dram", a.shape, _mybir.dt.from_np(a.dtype), kind="ExternalInput").ap())
    f = _rotary_frequencies()
    arrays["rotary_frequencies_dram"] = f
    args.append(nc.dram_tensor("rotary_frequencies_dram", f.shape, _mybir.dt.from_np(f.dtype), kind="ExternalInput").ap())
    for i, (shape, dtype) in enumerate(_OUTS):
        dt = _mybir.dt.from_np(_np.dtype(dtype))
        args.append(nc.dram_tensor(f"out_{i}_dram", shape, dt, kind="ExternalOutput").ap())
    block_kernel(nc, *args)
    r = _run(nc, [arrays], core_ids=[0])
    got = tuple(r.results[0][f"out_{i}_dram"] for i in range(len(_OUTS)))
    return got[0]
```

```python
from contextlib import ExitStack

import concourse.bass as bass
from concourse import mybir
import numpy as np

F32 = mybir.dt.float32
F16 = mybir.dt.float16
U32 = mybir.dt.uint32
ALU = mybir.AluOpType
ACT = mybir.ActivationFunctionType
AX_X = mybir.AxisListType.X

P = 128
B, T, DIM = 4, 512, 128
H, KV, HD, NODES = 16, 4, 64, 4
TB = T // P
HP = H + 1
PAIRS = H // 2
HALF = HD // 2
E, HID = 8, 512
BLOCKS = 6
UNITS_PER_B = 4 * H + 2
QKV = (H + 2 * KV) * HD
K0, V0 = H * HD, (H + KV) * HD
BIG = 32768.0
MAGIC = 12582912.0
TWO_PI_HI = 6.28125
TWO_PI_LO = 0.0019353071795864769
PI_CLAMP = 3.1415925
EPS = 1e-5
PTS_PER_B = 4 * H + 2


def block_kernel(nc, x, wq, wk, wv, wr, wo, w_router, w_up, w_gate, w_down, ws_up, ws_gate, ws_down,
                 c, wmod, inv_freq, out):
    ctx = ExitStack()
    with ctx:
        def sb(name, shape, dt=F32):
            return ctx.enter_context(nc.sbuf_tensor(name, shape, dt))

        def sem(name):
            return ctx.enter_context(nc.semaphore(name))

        ctx.enter_context(nc.allow_non_contiguous_dma(reason="small transposed loads"))
        psum = ctx.enter_context(nc.psum_tensor("psum", [P, 8, 512], F32))
        bank = [psum[:, i, :] for i in range(8)]
        psS = bank[0:4]
        psT0, psT1, psPT, psY = bank[4], bank[5], bank[6], bank[7]
        psT16 = [t_[:, :].bitcast(F16) for t_ in (psT0, psT1)]

        ident = sb("ident", [P, P])
        ident16 = sb("ident16", [P, P], F16)
        identbig = sb("identbig", [P, P], F16)
        causal = sb("causal", [P, P], F16)
        before = sb("before", [P, P], F16)
        ones16 = sb("ones16", [P, P], F16)
        headsel = sb("headsel", [P, HP])
        row64 = sb("row64", [P, 1])
        ones8 = sb("ones8", [E, P])
        half_pi = sb("half_pi", [P, 1])
        freq = sb("freq", [P, HALF])
        rank8 = sb("rank8", [P, E])

        w_qkv = sb("w_qkv", [P, QKV])
        w_r = sb("w_r", [P, H * NODES])
        w_o = sb("w_o", [P, PAIRS, DIM])
        w_rt = sb("w_rt", [P, E])

        c_t = sb("c_t", [P, B])
        c_e = sb("c_e", [P, B])
        c_s = sb("c_s", [P, B])
        mod = sb("mod", [P, 6, B])
        gsign = sb("gsign", [P, 2, B])
        gmag = sb("gmag", [P, 2, B])

        xb = sb("xb", [P, TB, DIM])
        stats = sb("stats", [P, TB, 6])
        mv = sb("mv", [P, TB, 2])
        ve = sb("ve", [P, TB])
        sd = sb("sd", [P, TB])
        rs = sb("rs", [P, 3, TB])
        xn = sb("xn", [P, TB, DIM])
        hT = sb("hT", [P, T])
        qkv = sb("qkv", [P, TB, QKV])
        lg = sb("lg", [P, TB, H, NODES])
        lmax = sb("lmax", [P, 2, TB * H])
        ew = sb("ew", [P, TB, H, NODES])
        member = sb("member", [P, TB, H, NODES])
        member16 = sb("member16", [P, TB, H, NODES], F16)
        sel = sb("sel", [P, TB, HP, 2, NODES])
        sel16 = sb("sel16", [P, 2, TB, H * NODES], F16)
        pairs = sb("pairs", [P, TB, HP, BLOCKS, 2], F16)
        prod = sb("prod", [P, TB * H, 2, NODES])
        es = sb("es", [P, TB * H, 2])
        wslot = sb("wslot", [P, TB, H, 2])
        slot = sb("slot", [P, TB * H, 2])
        cosn = sb("cosn", [P, TB, HP, 2, HALF])
        sinn = sb("sinn", [P, TB, HP, 2, HALF])

        pc = [sb(f"pc{s}", [P, TB, 2, HD]) for s in range(2)]
        ps = [sb(f"ps{s}", [P, TB, 2, HD]) for s in range(2)]
        gt, sc = [ps[i][:, :, :, :].rearrange("p t j d -> p (t j d)")[:, 0:6 * TB * H].rearrange(
            "p (k a) -> p k a", k=6) for i in range(2)]
        rot = pc
        sizes = [BLOCKS * T, 2 * NODES * T, 2 * NODES * T, 2 * TB * 2 * 5 * HD, TB * BLOCKS * P]
        ends = [sum(sizes[:i]) for i in range(len(sizes) + 1)]
        work = sb("work", [P, ends[-1]], F16)
        part = [work[:, ends[i]:ends[i + 1]] for i in range(len(sizes))]
        qT = part[0].rearrange("p (j t) -> p j t", j=BLOCKS)
        kT = part[1].rearrange("p (u n t) -> p u n t", u=2, n=NODES)
        klT = part[2].rearrange("p (u n t) -> p u n t", u=2, n=NODES)
        tile = part[3].rearrange("p (u t s k c) -> p u t s k c", u=2, t=TB, s=2, k=5)
        diag = part[4].rearrange("p (t j c) -> p t j c", t=TB, j=BLOCKS)
        mkq = sb("mkq", [P, 3, T], F16)
        mq = sb("mq", [P, 2, 2, T], F16)

        negmax = [sb(f"negmax{g}", [P, 2]) for g in range(2)]
        probs = [sb(f"probs{g}", [P, 2, T]) for g in range(2)]
        den = [sb(f"den{g}", [P, 2]) for g in range(2)]
        rden = [sb(f"rden{g}", [P, 2]) for g in range(2)]
        coef = [sb(f"coef{g}", [P, 2]) for g in range(2)]
        acc = [sb(f"acc{g}", [P, T]) for g in range(2)]
        accT_all = sb("accT", [P, 2, TB, T])
        accT = [accT_all[:, u, :, :] for u in range(2)]
        v_b = sb("v_b", [P, TB, HD])
        yT = sb("yT", [P, PAIRS + 1, T])

        chunks = [(0, 1), (1, 3), (3, 5), (5, PAIRS)]
        RED = int(np.sum(_rotary_frequencies()[0] * (T - 1) >= 3.14))
        ang_flat = accT_all[:, :, :, :].rearrange("p u j t -> p (u j t)")
        red_flat = yT[:, :, :].rearrange("p c t -> p (c t)")
        ang = [ang_flat[:, p0 * 4 * TB * HALF:p1 * 4 * TB * HALF].rearrange("p (t a f) -> p t a f", t=TB, f=HALF)
               for p0, p1 in chunks]
        red = [red_flat[:, 0:(p1 - p0) * 4 * TB * RED].rearrange("p (a f) -> p a f", f=RED) for p0, p1 in chunks]

        x1 = sb("x1", [P, B * TB, DIM])
        h2T = sb("h2T", [P, B * T])
        rl = sb("rl", [P, TB, E])
        rr = sb("rr", [P, 4, TB, E])
        rm = sb("rm", [P, 4, TB])
        ecoef = sb("ecoef", [P, B * TB, E])
        att = xn[:, :, :].rearrange("p t d -> p (t d)")
        w_mod = probs[0][:, :, :].rearrange("p e t -> p (e t)")[:, 0:6 * DIM]
        w_e = [qkv[:, i, :].rearrange("p (k n) -> p k n", k=3) for i in range(2)]
        cos_flat = cosn[:, :, :, :, :].rearrange("p t h s f -> p (t h s f)")
        sin_flat = sinn[:, :, :, :, :].rearrange("p t h s f -> p (t h s f)")
        ffnT = cos_flat[:, 0:B * T]
        crow = cos_flat[0:E, B * T:2 * B * T]
        coefT = sin_flat[0:E, 0:B * T]
        hidden = [sin_flat[:, 2048 + 512 * i:2560 + 512 * i] for i in range(2)]
        gateb = [sin_flat[:, 3072 + 512 * i:3584 + 512 * i] for i in range(2)]
        bc = [ps[i][:, :, :, :].rearrange("p t j d -> p (t j d)") for i in range(2)]
        wtd = [pc[i][:, :, :, :].rearrange("p t j d -> p (t j d)") for i in range(2)]

        names = """loaded x_in w_in w_slot0 w_slot1 out_done const_done ident_done init_done
            c_exp c_sum c_rec c_silu mod_mm mod_raw mod_one mod_sign mod_mag mod_done
            bn_s bn_a var_e std_dev rs_0 rs_1 rs_2 rs_3 xn_done xn_t h_ready proj_mm qkv_ev lg_mm
            rank_g rank_s rank_m l_max l_sub l_exp l_mem l_sum l_rec w_done mem16 pos_mm slots_w
            ang_mul ang_k ang_n ang_r1 ang_r2 ang_clamp ang_abs trig_sin trig_cos
            pc_done ps_done rot_done hi_done lo_done dup_done diag_done mq_done
            sel_a sel_b sel_cp pr_w es_done es_sum pe_passed mk_t mk_ev row_done head_sel pr_pos
            t_done t_ev kl_ev scores_done negmax_done exp_done rden_done coef_done acc_done
            pt_done pt_ev pv_done y_ev vb_done
            wo_mm att_ev att_t x1_done x1_kept passed r_mm r_ev r_max r_sub r_exp r_eq r_rk r_rm r_sum r_rec r_c r_cT r_cTev r_cev
            h2_ev h2_copy crow_done bc_mm bc_ev gu_mm silu_done hid_done down_mm wtd_done ffn_acc hid_used
            fin_g fin_t fin_done""".split()
        S = {n: sem(n) for n in names}

        kv_of = lambda h: K0 + (h // (H // KV)) * HD

        def step_no(b, h, s):
            return b * (4 * H) + h * 4 + s

        def rot_no(b, h):
            return b * HP + h

        def pt_no(b, h, ib):
            return b * PTS_PER_B + 2 + h * 4 + ib

        def unit_no(b, h, tb):
            return b * UNITS_PER_B + h * 4 + tb

        def unit_at(h, u, s):
            return (h, u, s + 2) if s < 2 else (h + 1, 1 - u, s - 2)

        def rows_at(h, u, s):
            return (h - 1, 1 - u, s + 2) if s < 2 else (h, u, s - 2)

        block = ctx.enter_context(nc.Block())

        @block.sync
        def _(sp):
            n_small = 0
            for dst, src in ((freq[:, :], inv_freq), (c_t[:, :], c.rearrange("b d -> d b")),
                             (w_mod[:, :], wmod), (w_qkv[:, 0:K0], wq), (w_qkv[:, K0:V0], wk),
                             (w_qkv[:, V0:QKV], wv), (w_r[:, :], wr),
                             (w_o[:, :, :], wo.rearrange("(c p) n -> p c n", p=P)), (w_rt[:, :], w_router)):
                sp.dma_start(dst, src).then_inc(S["loaded"], 16)
                n_small += 1
            with sp.Fori(0, B) as b:
                sp.wait_ge(S["x1_kept"], 1 + b)
                sp.dma_start(xb[:, :, :], x[bass.ds(b, 1), :, :].rearrange("a (t p) d -> p (a t) d", p=P)
                             ).then_inc(S["x_in"], 16)

        def load_expert(eng, i, up, gate, down):
            eng.dma_start(w_e[i][:, 0, :], up).then_inc(S[f"w_slot{i}"], 16)
            eng.dma_start(w_e[i][:, 1, :], gate).then_inc(S[f"w_slot{i}"], 16)
            eng.dma_start(w_e[i][:, 2, :].rearrange("p (c n) -> p c n", c=4),
                          down.rearrange("(c p) n -> p c n", p=P)).then_inc(S[f"w_slot{i}"], 16)

        @block.sync
        def _(sp):
            sp.wait_ge(S["wo_mm"], B)
            load_expert(sp, 0, ws_up, ws_gate, ws_down)
            load_expert(sp, 1, w_up[0], w_gate[0], w_down[0])
            with sp.Fori(0, 3) as r:
                for i in range(2):
                    e = r * 2 + 1 + i
                    sp.wait_ge(S["down_mm"], (r * 2 + 1 + i) * 4)
                    load_expert(sp, i, w_up[bass.ds(e, 1)].rearrange("a p n -> (a p) n"),
                                w_gate[bass.ds(e, 1)].rearrange("a p n -> (a p) n"),
                                w_down[bass.ds(e, 1)].rearrange("a p n -> (a p) n"))
            for b in range(B):
                sp.wait_ge(S["fin_done"], b + 1)
                sp.dma_start(out[b].rearrange("(t p) d -> p t d", p=P),
                             x1[:, b * TB:(b + 1) * TB, :]).then_inc(S["out_done"], 16)
            sp.wait_ge(S["out_done"], 16 * B)

        @block.gpsimd
        def _(pool):
            for t_, v in ((ident, 0.0), (ident16, 0.0), (identbig, 0.0), (causal, 0.0), (before, 1.0),
                          (ones16, 1.0), (headsel, 1.0), (row64, 0.0), (ones8, 1.0),
                          (half_pi, float(np.pi / 2))):
                pool.memset(t_[:, :], v).then_inc(S["const_done"], 1)
            pool.iota(rank8[:, :], [[-1, E]], base=E, channel_multiplier=0,
                      allow_small_or_imprecise_dtypes=True).then_inc(S["const_done"], 1)
            for u in range(2):
                pool.memset(acc[u][:, :], 0.0).then_inc(S["init_done"], 1)
                pool.memset(accT[u][:, :, :], 0.0).then_inc(S["init_done"], 1)
            pool.memset(mkq[:, 0, :], BIG).then_inc(S["init_done"], 1)
            pool.memset(mkq[:, 1:3, :], -BIG).then_inc(S["init_done"], 1)
            pool.memset(v_b[:, :, :], 0.0).then_inc(S["init_done"], 1)
            pool.memset(cosn[:, :, H, :, :], 0.0).then_inc(S["init_done"], 1)
            pool.memset(sinn[:, :, H, :, :], 0.0).then_inc(S["init_done"], 1)
            pool.memset(sel[:, :, :, :, :], 0.0).then_inc(S["init_done"], 1)
            pool.memset(pairs[:, :, :, :, :], 0.0).then_inc(S["init_done"], 1)
            pool.wait_ge(S["const_done"], 11)
            for t_, v in ((ident, 1.0), (ident16, 1.0), (identbig, BIG)):
                pool.affine_select(out=t_[:, :], in_=t_[:, :], compare_op=ALU.not_equal, fill=v, base=0,
                                   pattern=[[-1, P]], channel_multiplier=1).then_inc(S["ident_done"], 1)
            pool.affine_select(out=row64[:, :], in_=row64[:, :], compare_op=ALU.not_equal, fill=1.0, base=-HD,
                               pattern=[[0, 1]], channel_multiplier=1).then_inc(S["ident_done"], 1)
            pool.affine_select(out=headsel[:, :], in_=headsel[:, :], compare_op=ALU.is_ge, fill=0.0, base=0,
                               pattern=[[-NODES, HP]], channel_multiplier=1).then_inc(S["row_done"], 1)
            pool.affine_select(out=causal[:, :], in_=causal[:, :], compare_op=ALU.is_ge, fill=-BIG, base=0,
                               pattern=[[-1, P]], channel_multiplier=1).then_inc(S["ident_done"], 1)
            pool.affine_select(out=before[:, :], in_=before[:, :], compare_op=ALU.is_gt, fill=0.0, base=0,
                               pattern=[[1, P]], channel_multiplier=-1).then_inc(S["ident_done"], 1)

            pool.wait_ge(S["row_done"], 1)
            pool.affine_select(out=headsel[:, :], in_=headsel[:, :], compare_op=ALU.is_ge, fill=0.0,
                               base=NODES - 1, pattern=[[NODES, HP]], channel_multiplier=-1
                               ).then_inc(S["ident_done"], 1)

            pool.sem_inc(S["lo_done"], 1)

            def half_views(s, j):
                return [v[s][:, :, j, :].rearrange("p t (a f) -> p t a f", a=2) for v in (pc, ps)]

            def rotate_head(b, h, u, pair):
                r = rot_no(b, h)
                pool.wait_ge(S["trig_cos"], b * PAIRS + pair + 1)
                pool.wait_ge(S["qkv_ev"], (b + 1) * TB * 3)
                pool.wait_ge(S["hi_done"], 1 + r * 2)
                pool.wait_ge(S["lo_done"], 1 + r * 2)
                for s in range(2):
                    cs, sn = [v[:, :, bass.ds(h, 1), s, :] for v in (cosn, sinn)]
                    for j, col in ((0, h * HD), (1, kv_of(h))):
                        src = qkv[:, :, bass.ds(col, HD)].rearrange("p t (a f) -> p t a f", a=2)
                        pool.tensor_tensor(half_views(s, j)[0], src, cs.to_broadcast([P, TB, 2, HALF]), ALU.mult
                                           ).then_inc(S["pc_done"], 1)
                        for half in range(2):
                            pool.tensor_tensor(ps[s][:, :, j, half * HALF:(half + 1) * HALF],
                                               qkv[:, :, bass.ds(col + (1 - half) * HALF, HALF)],
                                               sn.rearrange("p t a f -> p t (a f)"), ALU.mult
                                               ).then_inc(S["ps_done"], 1)
                for s in range(2):
                    pool.wait_ge(S["pc_done"], r * 4 + s * 2 + 2)
                    pool.wait_ge(S["ps_done"], r * 8 + s * 4 + 4)
                    for half, op in ((0, ALU.subtract), (1, ALU.add)):
                        sl = slice(half * HALF, (half + 1) * HALF)
                        pool.tensor_tensor(rot[s][:, :, :, sl], pc[s][:, :, :, sl], ps[s][:, :, :, sl], op
                                           ).then_inc(S["rot_done"], 1)
                pool.wait_ge(S["rot_done"], r * 4 + 4)
                for s in range(2):
                    pool.wait_ge(S["hi_done"], 1 + r * 2 + s + 1)
                    pool.tensor_tensor(tile[:, u, :, s, 1:5:3, :], rot[s][:, :, :, :], tile[:, u, :, s, 0:3:2, :],
                                       ALU.subtract).then_inc(S["lo_done"], 1)

            with pool.Fori(0, B) as b:
                with pool.Fori(0, PAIRS) as hp:
                    for u in range(2):
                        rotate_head(b, hp * 2 + u, u, hp)
                rotate_head(b, H, 0, PAIRS - 1)

        @block.scalar
        def _(act):
            act.wait_ge(S["loaded"], 16 * 9)
            act.activation(c_e[:, :], c_t[:, :], ACT.Exp, scale=-1.0).then_inc(S["c_exp"], 1)
            act.sem_inc(S["exp_done"], 3)
            for name in ("t_ev", "pt_ev", "y_ev", "vb_done"):
                act.sem_inc(S[name], 1)

            def norm_and_project(b, turn, which):
                act.wait_ge(S["var_e"], turn + 1)
                act.activation(sd[:, :], ve[:, :], ACT.Sqrt).then_inc(S["std_dev"], 1)
                act.wait_ge(S["xn_t"], turn + 1)
                act.wait_ge(S["mod_done"], 3)
                act.activation(hT[:, :], psPT[:, :], ACT.Identity,
                               bias=mod[:, which, bass.ds(b, 1)], scale=mod[:, which + 1, bass.ds(b, 1)]
                               ).then_inc(S["h_ready"], 1)

            def move_pt(b, h, u, ib):
                act.wait_ge(S["pt_done"], pt_no(b, h, ib) + 1)
                w = ib + 1
                act.activation(accT[u][:, 0:w, ib * P:(ib + 1) * P],
                               psPT[:, 0:w * P].rearrange("p (j i) -> p j i", j=w), ACT.Copy
                               ).then_inc(S["pt_ev"], 1)

            def keep_q(b, h, tb):
                m, rows = unit_no(b, h, tb), slice(tb * P, (tb + 1) * P)
                for j, bank_ in enumerate((psT0, psT1)):
                    act.wait_ge(S["t_done"], m * 4 + j + 1)
                    act.activation(qT[:, 3 * j:3 * j + 3, rows], bank_[:, 0:3 * P].rearrange("p (j t) -> p j t", j=3),
                                   ACT.Copy).then_inc(S["t_ev"], 1)

            def keep_k(b, h, u, tb):
                m = unit_no(b, h, tb)
                act.wait_ge(S["t_done"], m * 4 + 3)
                act.activation(kT[:, u, :, tb * P:(tb + 1) * P], psT0[:, :].rearrange("p (n t) -> p n t", n=NODES),
                               ACT.Copy).then_inc(S["t_ev"], 1)

            with act.Fori(0, B) as b:
                norm_and_project(b, b * 2, 0)
                for tb in range(TB):
                    act.wait_ge(S["proj_mm"], b * TB + tb + 1)
                    for j, i in enumerate((0, 1, 2) if tb % 2 == 0 else (4, 5, 7)):
                        act.activation(qkv[:, tb, j * 512:(j + 1) * 512], bank[i][:, :], ACT.Copy,
                                       scale=HD ** -0.5 if j < 2 else 1.0).then_inc(S["qkv_ev"], 1)
                    if tb == 1:
                        act.wait_ge(S["l_sub"], b + 1)
                        act.activation(ew[:, :, :, :], ew[:, :, :, :], ACT.Exp).then_inc(S["l_exp"], 1)
                        act.preload_act_table(ACT.Sin)

                def trigonometry(i):
                    p0, p1 = chunks[i]
                    heads = slice(2 * p0, 2 * p1)
                    a_ = ang[i].rearrange("p t a f -> p t (a f)")
                    act.wait_ge(S["ang_clamp"], b * len(chunks) + i + 1)
                    act.activation(sinn[:, :, heads, :, :].rearrange("p t h s f -> p t (h s f)"), a_, ACT.Sin
                                   ).then_inc(S["trig_sin"], 1)
                    act.activation(a_, a_, ACT.Abs).then_inc(S["ang_abs"], 1)
                    act.wait_ge(S["ang_abs"], b * len(chunks) + i + 1)
                    act.activation(cosn[:, :, heads, :, :].rearrange("p t h s f -> p t (h s f)"), a_, ACT.Sin,
                                   scale=-1.0, bias=half_pi[:, 0:1]).then_inc(S["trig_cos"], p1 - p0)

                for i in range(len(chunks) - 1):
                    trigonometry(i)
                act.wait_ge(S["mk_t"], b + 1)
                act.activation(mkq[0:HD, 0:2, :].rearrange("p k t -> p (k t)"), psT16[0][0:HD, :], ACT.Copy,
                               scale=BIG).then_inc(S["mk_ev"], 1)
                act.activation(mkq[0:HD, 2, :], psT16[1][0:HD, 0:T], ACT.Copy, scale=BIG).then_inc(S["mk_ev"], 1)
                for tb in range(2):
                    keep_q(b, 0, tb)
                    keep_k(b, 0, 0, tb)
                trigonometry(len(chunks) - 1)
                act.preload_act_table(ACT.Exp)
                with act.Fori(0, PAIRS) as hp:
                    for u in range(2):
                        h = hp * 2 + u
                        for s in range(TB):
                            w, g = (s + 1) * P, s % 2
                            k = step_no(b, h, s)
                            uh, uu, tb = unit_at(h, u, s)
                            keep_q(b, uh, tb)
                            keep_k(b, uh, uu, tb)
                            act.wait_ge(S["negmax_done"], k + 1)
                            act.wait_ge(S["acc_done"], 1 + k * 2)
                            for e in range(2):
                                act.activation(probs[g][:, e, 0:w], psS[2 * g + e][:, 0:w], ACT.Exp,
                                               bias=negmax[g][:, e:e + 1], accum_out=den[g][:, e:e + 1]
                                               ).then_inc(S["exp_done"], 1)
                            if u == 0 and s == 2:
                                act.wait_ge(S["pv_done"], b * (PAIRS + 1) + hp + 1)
                                act.activation(yT[:, bass.ds(hp, 1), :].rearrange("p a t -> p (a t)"),
                                               psY[:, :], ACT.Copy).then_inc(S["y_ev"], 1)
                                act.activation(v_b[:, :, :], qkv[:, :, bass.ds((hp // 2) * HD + V0, HD)],
                                               ACT.Copy).then_inc(S["vb_done"], 1)
                            move_pt(b, *rows_at(h, u, s))
                move_pt(b, H - 1, 1, 2)
                move_pt(b, H - 1, 1, 3)
                act.wait_ge(S["pv_done"], (b + 1) * (PAIRS + 1))
                act.activation(yT[:, PAIRS, :], psY[:, :], ACT.Copy).then_inc(S["y_ev"], 1)
                act.wait_ge(S["wo_mm"], b + 1)
                act.activation(att[:, :], psPT[:, :], ACT.Copy, scale=mod[:, 2, bass.ds(b, 1)]
                               ).then_inc(S["att_ev"], 1)
                norm_and_project(b, b * 2 + 1, 3)
                act.wait_ge(S["h_ready"], b * 2 + 2)
                act.activation(h2T[:, bass.ds(b * T, T)], hT[:, :], ACT.Copy).then_inc(S["h2_copy"], 1)
                act.wait_ge(S["r_sub"], b + 1)
                act.activation(rr[:, 0, :, :], rr[:, 0, :, :], ACT.Exp).then_inc(S["r_exp"], 1)

            def gates(n0):
                for i in range(16):
                    n = n0 + i
                    act.wait_ge(S["gu_mm"], n + 1)
                    act.wait_ge(S["hid_done"], n)
                    act.activation(gateb[i % 2][:, :], bank[i % 2][:, :], ACT.Silu).then_inc(S["silu_done"], 1)

            gates(0)
            gates(16)
            with act.Fori(0, 3) as r:
                gates(r * 32 + 32)
                gates(r * 32 + 48)
            for b in range(B):
                act.wait_ge(S["ffn_acc"], 32)
                act.activation(ffnT[:, b * T:(b + 1) * T], ffnT[:, b * T:(b + 1) * T], ACT.Copy,
                               scale=mod[:, 5, b:b + 1]).then_inc(S["fin_g"], 1)

        @block.vector
        def _(dve):
            dve.wait_ge(S["c_exp"], 1)
            dve.tensor_scalar(c_e[:, :], c_e[:, :], 1.0, None, ALU.add).then_inc(S["c_sum"], 1)
            dve.wait_ge(S["c_sum"], 1)
            dve.reciprocal(c_s[:, :], c_e[:, :]).then_inc(S["c_rec"], 1)
            dve.wait_ge(S["c_rec"], 1)
            dve.tensor_tensor(c_s[:, :], c_s[:, :], c_t[:, :], ALU.mult).then_inc(S["c_silu"], 1)
            dve.wait_ge(S["mod_mm"], 1)
            dve.tensor_copy(mod[:, :, :].rearrange("p a b -> p (a b)"), psT0[:, 0:6 * B]).then_inc(S["mod_raw"], 1)
            dve.wait_ge(S["mod_raw"], 1)
            for j in range(2):
                dve.tensor_scalar(mod[:, 3 * j + 1, :], mod[:, 3 * j + 1, :], 1.0, None, ALU.add
                                  ).then_inc(S["mod_done"], 1)
            g_raw = mod[:, :, :].rearrange("p (j k) b -> p j k b", j=2)[:, :, 2, :]
            dve.tensor_scalar(gsign[:, :, :], g_raw, 0.0, 2.0, ALU.is_ge, ALU.mult).then_inc(S["mod_sign"], 1)
            dve.scalar_tensor_tensor(gmag[:, :, :], g_raw, -1.0, g_raw, ALU.mult, ALU.max).then_inc(S["mod_sign"], 1)
            dve.wait_ge(S["mod_sign"], 2)
            dve.tensor_scalar(gmag[:, :, :], gmag[:, :, :], 0.25, None, ALU.max).then_inc(S["mod_mag"], 1)
            dve.wait_ge(S["mod_mag"], 1)
            dve.scalar_tensor_tensor(g_raw, gsign[:, :, :], -1.0, gmag[:, :, :], ALU.add, ALU.mult
                                     ).then_inc(S["mod_done"], 1)

            def layer_norm(turn):
                for tb in range(TB):
                    dve.bn_stats(stats[:, tb, :], xb[:, tb, :]).then_inc(S["bn_s"], 1)
                dve.wait_ge(S["bn_s"], (turn + 1) * TB)
                dve.sem_inc(S["passed"], 1)
                for tb in range(TB):
                    dve.bn_aggr(mv[:, tb, :], stats[:, tb, :]).then_inc(S["bn_a"], 1)
                dve.wait_ge(S["bn_a"], (turn + 1) * TB)
                dve.tensor_scalar(ve[:, :], mv[:, :, 1], EPS, None, ALU.add).then_inc(S["var_e"], 1)
                dve.wait_ge(S["std_dev"], turn + 1)
                dve.reciprocal(rs[:, 0, :], sd[:, :]).then_inc(S["rs_0"], 1)
                dve.wait_ge(S["rs_0"], turn + 1)
                dve.tensor_tensor(rs[:, 1, :], rs[:, 0, :], rs[:, 0, :], ALU.mult).then_inc(S["rs_1"], 1)
                dve.wait_ge(S["rs_1"], turn + 1)
                dve.scalar_tensor_tensor(rs[:, 2, :], rs[:, 1, :], -0.5, ve[:, :], ALU.mult, ALU.mult
                                         ).then_inc(S["rs_2"], 1)
                dve.wait_ge(S["rs_2"], turn + 1)
                dve.scalar_tensor_tensor(rs[:, 1, :], rs[:, 2, :], 1.5, rs[:, 0, :], ALU.add, ALU.mult
                                         ).then_inc(S["rs_3"], 1)
                dve.wait_ge(S["rs_3"], turn + 1)
                for tb in range(TB):
                    dve.tensor_scalar(xn[:, tb, :], xb[:, tb, :], mv[:, tb, 0:1], rs[:, 1, tb:tb + 1],
                                      ALU.subtract, ALU.mult).then_inc(S["xn_done"], 1)

            def high(b, h, u):
                r = rot_no(b, h)
                for s in range(2):
                    dve.wait_ge(S["rot_done"], r * 4 + s * 2 + 2)
                    dve.tensor_copy(tile[:, u, :, s, 0:3:2, :], rot[s][:, :, :, :]).then_inc(S["hi_done"], 1)

            def double(b, h, u):
                dve.wait_ge(S["hi_done"], 1 + rot_no(b, h) * 2 + 2)
                dve.tensor_copy(tile[:, u, :, :, 3, :], tile[:, u, :, :, 2, :]).then_inc(S["dup_done"], 1)

            def diagonals(b, h, tb):
                r = rot_no(b, h)
                dve.tensor_tensor(
                    diag[:, tb, :, :].rearrange("p j (c k) -> p j c k", k=2),
                    ident16[:, :].rearrange("p (c k) -> p c k", k=2).unsqueeze(1).to_broadcast([P, BLOCKS, P // 2, 2]),
                    pairs[:, tb, bass.ds(h, 1), :, :].rearrange("p a j k -> p (a j) k").unsqueeze(2).to_broadcast(
                        [P, BLOCKS, P // 2, 2]), ALU.mult).then_inc(S["diag_done"], 1)

            def query_masks(b, h, u):
                dve.tensor_scalar(mq[0:HD + 1, u, :, :], mkq[0:HD + 1, 1:3, :],
                                  headsel[0:HD + 1, bass.ds(h, 1)] if not isinstance(h, int)
                                  else headsel[0:HD + 1, h:h + 1], None, ALU.mult).then_inc(S["mq_done"], 1)

            def keep_kl(b, h, u, tb):
                m = unit_no(b, h, tb)
                dve.wait_ge(S["t_done"], m * 4 + 4)
                dve.tensor_copy(klT[0:HD, u, :, tb * P:(tb + 1) * P],
                                psT1[0:HD, :].rearrange("p (n t) -> p n t", n=NODES)).then_inc(S["kl_ev"], 1)

            def inverse_sums(b, h, s):
                dve.wait_ge(S["exp_done"], 3 + step_no(b, h, s) * 2 + 2)
                dve.reciprocal(rden[s % 2][:, :], den[s % 2][:, :]).then_inc(S["rden_done"], 1)

            def coefficients(b, h, s):
                g = s % 2
                dve.wait_ge(S["rden_done"], step_no(b, h, s) + 1)
                dve.tensor_tensor(coef[g][:, :], rden[g][:, :],
                                  wslot[:, s, bass.ds(h, 1), :].rearrange("p a n -> p (a n)"), ALU.mult
                                  ).then_inc(S["coef_done"], 1)

            def weigh_a(b, h, s):
                k, g, w = step_no(b, h, s), s % 2, (s + 1) * P
                dve.wait_ge(S["coef_done"], k + 1)
                dve.wait_ge(S["pt_done"], pt_no(b, h, s) - 1)
                dve.tensor_scalar(acc[g][:, 0:w], probs[g][:, 0, 0:w], coef[g][:, 0:1], None, ALU.mult
                                  ).then_inc(S["acc_done"], 1)

            def weigh_b(b, h, s):
                k, g, w = step_no(b, h, s), s % 2, (s + 1) * P
                dve.wait_ge(S["acc_done"], 3 + k * 2 + 1)
                dve.scalar_tensor_tensor(acc[g][:, 0:w], probs[g][:, 1, 0:w], coef[g][:, 1:2], acc[g][:, 0:w],
                                         ALU.mult, ALU.add).then_inc(S["acc_done"], 1)

            dve.wait_ge(S["ident_done"], 7)
            dve.tensor_scalar(headsel[:, :], headsel[:, :], row64[:, 0:1], None, ALU.max).then_inc(S["head_sel"], 1)
            dve.wait_ge(S["head_sel"], 1)
            dve.sem_inc(S["kl_ev"], 1)
            dve.sem_inc(S["acc_done"], 3)
            dve.sem_inc(S["hi_done"], 1)
            dve.sem_inc(S["x1_kept"], 1)
            dve.wait_ge(S["ident_done"], 7)
            dve.wait_ge(S["init_done"], 11)
            with dve.Fori(0, B) as b:
                dve.wait_ge(S["x_in"], (b + 1) * 16)
                layer_norm(b * 2)
                dve.wait_ge(S["lg_mm"], b + 1)
                dve.tensor_copy(lg[:, :, :, :].rearrange("p t h n -> p (t h n)"), bank[3][:, 0:TB * H * NODES]
                                ).then_inc(S["rank_g"], 1)
                dve.wait_ge(S["rank_g"], b + 1)
                L = lg[:, :, :, :].rearrange("p t h n -> p (t h) n")
                M = member[:, :, :, :].rearrange("p t h n -> p (t h) n")
                W = ew[:, :, :, :].rearrange("p t h n -> p (t h) n")
                duo = [(0, 1), (0, 2), (0, 3), (1, 2), (1, 3), (2, 3)]
                for i, (m, n) in enumerate(duo):
                    dve.tensor_tensor(gt[:, i, :], L[:, :, m], L[:, :, n], ALU.is_ge).then_inc(S["rank_s"], 1)
                dve.tensor_reduce(lmax[:, 0, :], L, AX_X, ALU.max).then_inc(S["l_max"], 1)
                dve.wait_ge(S["l_max"], b + 1)
                dve.tensor_tensor(W, L, lmax[:, 0, :].unsqueeze(2).to_broadcast([P, TB * H, NODES]), ALU.subtract
                                  ).then_inc(S["l_sub"], 1)
                dve.wait_ge(S["rank_s"], (b + 1) * 6)
                for i, (a, c_, op) in enumerate(((0, 1, ALU.add), (3, 4, ALU.add), (5, 1, ALU.subtract),
                                                 (2, 4, ALU.add))):
                    dve.tensor_tensor(sc[:, i, :], gt[:, a, :], gt[:, c_, :], op).then_inc(S["rank_m"], 1)
                dve.wait_ge(S["rank_m"], b * 8 + 4)
                for i, a, op in ((0, 2, ALU.add), (1, 0, ALU.subtract), (2, 3, ALU.subtract), (3, 5, ALU.add)):
                    dve.tensor_tensor(sc[:, i, :], sc[:, i, :], gt[:, a, :], op).then_inc(S["rank_m"], 1)
                dve.wait_ge(S["rank_m"], b * 8 + 8)
                for n, (v, op) in enumerate(((1.5, ALU.is_gt), (0.5, ALU.is_gt), (-0.5, ALU.is_gt), (1.5, ALU.is_lt))):
                    dve.tensor_scalar(M[:, :, n], sc[:, n, :], v, None, op).then_inc(S["l_mem"], 1)
                dve.wait_ge(S["l_mem"], (b + 1) * 4)
                dve.tensor_copy(member16[:, :, :, :], member[:, :, :, :]).then_inc(S["mem16"], 1)
                sA, sB = sel[:, :, 0:H, 0, :], sel[:, :, 0:H, 1, :]
                Mb = lambda n: member[:, :, :, n]
                dve.tensor_copy(sA[:, :, :, 0], Mb(0)).then_inc(S["sel_a"], 1)
                dve.tensor_tensor(sA[:, :, :, 1], Mb(1), Mb(0), ALU.is_gt).then_inc(S["sel_a"], 1)
                dve.tensor_tensor(sA[:, :, :, 2], Mb(2), Mb(3), ALU.mult).then_inc(S["sel_a"], 1)
                dve.wait_ge(S["sel_a"], (b + 1) * 3)
                dve.tensor_tensor(sB, member[:, :, :, :], sA, ALU.subtract).then_inc(S["sel_b"], 1)
                dve.wait_ge(S["sel_b"], b + 1)
                for i, v in enumerate((sA, sB)):
                    dve.tensor_copy(sel16[:, i, :, :].rearrange("p t (h n) -> p t h n", h=H), v
                                    ).then_inc(S["sel_cp"], 1)
                    dve.tensor_copy(
                        pairs[:, :, :, 3 * i:3 * i + 3, :].rearrange("p t h j k -> p (t h) j k"),
                        sel[:, :, :, i, i:i + 3].rearrange("p t h j -> p (t h) j").unsqueeze(3).to_broadcast(
                            [P, TB * HP, 3, 2])).then_inc(S["sel_cp"], 1)
                dve.wait_ge(S["pos_mm"], b + 1)
                pos = psPT[:, 0:TB * H * NODES].rearrange("p (t h n) -> p t h n", t=TB, h=H)
                PR = prod[:, :, :, :].rearrange("p (t h) i n -> p t h i n", t=TB)
                for i, v in enumerate((sA, sB)):
                    dve.tensor_tensor(PR[:, :, :, i, :], pos, v, ALU.mult).then_inc(S["pr_pos"], 1)
                dve.wait_ge(S["pr_pos"], (b + 1) * 2)
                dve.tensor_reduce(slot[:, :, :], prod[:, :, :, :], AX_X, ALU.add).then_inc(S["slots_w"], 1)
                dve.wait_ge(S["slots_w"], b + 1)

                def angles(i):
                    p0, p1 = chunks[i]
                    n = b * len(chunks) + i + 1
                    c0, c1 = 4 * p0, 4 * p1
                    a_, r_ = ang[i].rearrange("p t a f -> p (t a) f")[:, :, 0:RED], red[i]
                    p_ = slot[:, :, :].rearrange("p (t h) s -> p t (h s)", t=TB)[:, :, c0:c1]
                    dve.tensor_tensor(ang[i], p_.unsqueeze(3).to_broadcast([P, TB, c1 - c0, HALF]),
                                      freq[:, :].unsqueeze(1).unsqueeze(1).to_broadcast([P, TB, c1 - c0, HALF]),
                                      ALU.mult).then_inc(S["ang_mul"], 1)
                    dve.wait_ge(S["ang_mul"], n)
                    dve.tensor_scalar(r_, a_, float(1 / (2 * np.pi)), MAGIC, ALU.mult, ALU.add
                                      ).then_inc(S["ang_k"], 1)
                    dve.wait_ge(S["ang_k"], n)
                    dve.tensor_scalar(r_, r_, MAGIC, None, ALU.subtract).then_inc(S["ang_n"], 1)
                    dve.wait_ge(S["ang_n"], n)
                    dve.scalar_tensor_tensor(a_, r_, -TWO_PI_HI, a_, ALU.mult, ALU.add).then_inc(S["ang_r1"], 1)
                    dve.wait_ge(S["ang_r1"], n)
                    dve.scalar_tensor_tensor(a_, r_, -TWO_PI_LO, a_, ALU.mult, ALU.add).then_inc(S["ang_r2"], 1)
                    dve.wait_ge(S["ang_r2"], n)
                    dve.tensor_scalar(a_, a_, PI_CLAMP, -PI_CLAMP, ALU.min, ALU.max).then_inc(S["ang_clamp"], 1)

                for i in range(len(chunks) - 1):
                    angles(i)
                    if i == 0:
                        dve.wait_ge(S["sel_cp"], (b + 1) * 4)
                        for tb in range(TB):
                            diagonals(b, 0, tb)
                dve.wait_ge(S["l_exp"], b + 1)
                for i, v in enumerate((sA, sB)):
                    dve.tensor_tensor(PR[:, :, :, i, :], ew[:, :, :, :], v, ALU.mult).then_inc(S["pr_w"], 1)
                dve.wait_ge(S["pr_w"], (b + 1) * 2)
                dve.tensor_reduce(es[:, :, :], prod[:, :, :, :], AX_X, ALU.add).then_inc(S["es_done"], 1)
                dve.wait_ge(S["es_done"], b + 1)
                dve.tensor_tensor(lmax[:, 1, :], es[:, :, 0], es[:, :, 1], ALU.add).then_inc(S["es_sum"], 1)
                dve.wait_ge(S["es_sum"], b + 1)
                dve.reciprocal(lmax[:, 0, :], lmax[:, 1, :]).then_inc(S["l_rec"], 1)
                dve.wait_ge(S["l_rec"], b + 1)
                dve.tensor_tensor(wslot[:, :, :, :].rearrange("p t h s -> p (t h) s"), es[:, :, :],
                                  lmax[:, 0, :].unsqueeze(2).to_broadcast([P, TB * H, 2]), ALU.mult
                                  ).then_inc(S["w_done"], 1)
                high(b, 0, 0)
                double(b, 0, 0)
                dve.wait_ge(S["mk_ev"], (b + 1) * 2)
                query_masks(b, 0, 0)
                angles(len(chunks) - 1)
                for tb in range(2):
                    keep_kl(b, 0, 0, tb)
                with dve.Fori(0, PAIRS) as hp:
                    for u in range(2):
                        h = hp * 2 + u
                        for s in range(TB):
                            g, w = s % 2, (s + 1) * P
                            uh, uu, tb = unit_at(h, u, s)
                            last = (h, s - 1) if s else (h - 1, TB - 1)
                            weigh = not (u == 0 and s == 0)
                            dve.wait_ge(S["scores_done"], step_no(b, h, s) + 1)
                            dve.tensor_reduce(negmax[g][:, :], psum[:, 2 * g:2 * g + 2, 0:w], AX_X, ALU.max,
                                              negate=True).then_inc(S["negmax_done"], 1)
                            if weigh:
                                inverse_sums(b, *last)
                            diagonals(b, h + 1, s)
                            if weigh:
                                coefficients(b, *last)
                            if s == 1:
                                double(b, h + 1, 1 - u)
                            if weigh:
                                weigh_a(b, *last)
                            keep_kl(b, uh, uu, tb)
                            if weigh:
                                weigh_b(b, *last)
                            if s == 0:
                                high(b, h + 1, 1 - u)
                            if s == 1:
                                query_masks(b, h + 1, 1 - u)
                    inverse_sums(b, h, TB - 1)
                    coefficients(b, h, TB - 1)
                    weigh_a(b, h, TB - 1)
                    weigh_b(b, h, TB - 1)
                dve.wait_ge(S["att_t"], b + 1)
                dve.tensor_tensor(xb[:, :, :], psY[:, :].rearrange("p (t d) -> p t d", t=TB), xb[:, :, :], ALU.add
                                  ).then_inc(S["x1_done"], 1)
                dve.wait_ge(S["x1_done"], b + 1)
                layer_norm(b * 2 + 1)
                dve.tensor_copy(x1[:, bass.ds(b * TB, TB), :], xb[:, :, :]).then_inc(S["x1_kept"], 1)
                dve.wait_ge(S["r_mm"], b + 1)
                dve.tensor_copy(rl[:, :, :].rearrange("p t e -> p (t e)"), psT0[:, 0:TB * E]).then_inc(S["r_ev"], 1)
                dve.wait_ge(S["r_ev"], b + 1)
                dve.tensor_reduce(rm[:, 0, :], rl[:, :, :], AX_X, ALU.max).then_inc(S["r_max"], 1)
                dve.wait_ge(S["r_max"], b + 1)
                top = rm[:, 0, :].unsqueeze(2).to_broadcast([P, TB, E])
                dve.tensor_tensor(rr[:, 0, :, :], rl[:, :, :], top, ALU.subtract).then_inc(S["r_sub"], 1)
                dve.tensor_tensor(rr[:, 1, :, :], rl[:, :, :], top, ALU.is_ge).then_inc(S["r_eq"], 1)
                dve.wait_ge(S["r_eq"], b + 1)
                dve.tensor_tensor(rr[:, 2, :, :], rr[:, 1, :, :], rank8[:, :].unsqueeze(1).to_broadcast([P, TB, E]),
                                  ALU.mult).then_inc(S["r_rk"], 1)
                dve.wait_ge(S["r_rk"], b + 1)
                dve.tensor_reduce(rm[:, 1, :], rr[:, 2, :, :], AX_X, ALU.max).then_inc(S["r_rm"], 1)
                dve.wait_ge(S["r_exp"], b + 1)
                dve.tensor_reduce(rm[:, 2, :], rr[:, 0, :, :], AX_X, ALU.add).then_inc(S["r_sum"], 1)
                dve.wait_ge(S["r_sum"], b + 1)
                dve.reciprocal(rm[:, 3, :], rm[:, 2, :]).then_inc(S["r_rec"], 1)
                dve.wait_ge(S["r_rm"], b + 1)
                dve.tensor_tensor(rr[:, 1, :, :], rr[:, 2, :, :], rm[:, 1, :].unsqueeze(2).to_broadcast([P, TB, E]),
                                  ALU.is_equal).then_inc(S["r_c"], 1)
                dve.wait_ge(S["r_c"], b * 2 + 1)
                dve.wait_ge(S["r_rec"], b + 1)
                dve.scalar_tensor_tensor(rr[:, 3, :, :], rr[:, 1, :, :], 2.0,
                                         rm[:, 3, :].unsqueeze(2).to_broadcast([P, TB, E]), ALU.mult, ALU.mult
                                         ).then_inc(S["r_c"], 1)
                dve.wait_ge(S["r_c"], b * 2 + 2)
                dve.tensor_copy(ecoef[:, bass.ds(b * TB, TB), :], rr[:, 3, :, :]).then_inc(S["r_cev"], 1)

            for t_ in range(B):
                dve.wait_ge(S["r_cT"], t_ + 1)
                dve.tensor_copy(coefT[:, t_ * T:(t_ + 1) * T], bank[4 + t_][0:E, :]).then_inc(S["r_cTev"], 1)
            dve.sem_inc(S["hid_done"], 1)

            def coef_row(m):
                dve.wait_ge(S["bc_mm"], (m - 1) * 4)
                dve.wait_ge(S["r_cTev"], B)
                dve.tensor_scalar(crow[:, :], coefT[:, :], ident[0:E, bass.ds(m - 1, 1)] if not isinstance(m, int)
                                  else ident[0:E, m - 1:m], None, ALU.mult).then_inc(S["crow_done"], 1)

            def hidden_and_sum(m, shared):
                n0 = m * 16
                if not shared:
                    coef_row(m)

                def total(t_):
                    o = t_ % 2
                    dst = ffnT[:, t_ * 512:(t_ + 1) * 512]
                    dve.wait_ge(S["down_mm"], m * 4 + t_ + 1)
                    if shared:
                        dve.tensor_copy(dst, bank[4 + o][:, :]).then_inc(S["ffn_acc"], 1)
                        return
                    dve.wait_ge(S["bc_mm"], (m - 1) * 4 + t_ + 1)
                    dve.tensor_copy(bc[o][:, :], bank[6 + o][:, :]).then_inc(S["bc_ev"], 1)
                    dve.wait_ge(S["bc_ev"], (m - 1) * 4 + t_ + 1)
                    dve.tensor_tensor(wtd[o][:, :], bank[4 + o][:, :], bc[o][:, :], ALU.mult
                                      ).then_inc(S["wtd_done"], 1)
                    dve.wait_ge(S["wtd_done"], (m - 1) * 4 + t_ + 1)
                    dve.wait_ge(S["ffn_acc"], m * 4 + t_ - 3)
                    dve.tensor_tensor(dst, dst, wtd[o][:, :], ALU.add).then_inc(S["ffn_acc"], 1)

                for t_ in range(B):
                    for c_ in range(4):
                        i = t_ * 4 + c_
                        dve.wait_ge(S["silu_done"], n0 + i + 1)
                        if not (shared and i < 2):
                            dve.wait_ge(S["hid_used"], n0 + i - 1)
                        dve.tensor_tensor(hidden[i % 2][:, :], bank[2 + i % 2][:, :], gateb[i % 2][:, :],
                                          ALU.mult).then_inc(S["hid_done"], 1)
                        if c_ == 1 and t_:
                            total(t_ - 1)
                total(3)

            hidden_and_sum(0, True)
            hidden_and_sum(1, False)
            with dve.Fori(0, 3) as r:
                hidden_and_sum(r * 2 + 2, False)
                hidden_and_sum(r * 2 + 3, False)
            for b in range(B):
                dve.wait_ge(S["fin_t"], b + 1)
                dve.tensor_tensor(x1[:, b * TB:(b + 1) * TB, :],
                                  bank[b % 2][:, :].rearrange("p (t d) -> p t d", t=TB),
                                  x1[:, b * TB:(b + 1) * TB, :], ALU.add).then_inc(S["fin_done"], 1)

        @block.tensor
        def _(pe):
            pe.wait_ge(S["c_silu"], 1)
            pe.wait_ge(S["loaded"], 16 * 9)
            for j in range(6):
                mm = pe.matmul(psT0[:, j * B:(j + 1) * B], w_mod[:, j * DIM:(j + 1) * DIM], c_s[:, :],
                               start=True, stop=True)
            mm.then_inc(S["mod_mm"], 1)
            pe.wait_ge(S["ident_done"], 7)
            pe.wait_ge(S["init_done"], 11)

            def norm_rows(turn):
                pe.wait_ge(S["xn_done"], (turn + 1) * TB)
                for tb in range(TB):
                    mm = pe.transpose(psPT[:, tb * P:(tb + 1) * P], xn[:, tb, :], ident[:, :])
                mm.then_inc(S["xn_t"], 1)

            def sort_q(b, h, u, tb):
                m, r = unit_no(b, h, tb), rot_no(b, h)
                pe.wait_ge(S["lo_done"], 1 + r * 2 + 2)
                pe.wait_ge(S["diag_done"], r * 4 + tb + 1)
                pe.wait_ge(S["t_ev"], 1 + m * 3)
                pe.matmul(psT0[:, 0:3 * P], tile[:, u, tb, 0, 0:2, :].rearrange("p k c -> p (k c)"),
                          diag[:, tb, 0:3, :].rearrange("p j c -> p (j c)"), start=True, stop=True
                          ).then_inc(S["t_done"], 1)
                pe.wait_ge(S["kl_ev"], 1 + m)
                pe.matmul(psT1[:, 0:3 * P], tile[:, u, tb, 1, 0:2, :].rearrange("p k c -> p (k c)"),
                          diag[:, tb, 3:6, :].rearrange("p j c -> p (j c)"), start=True, stop=True
                          ).then_inc(S["t_done"], 1)

            def sort_k(b, h, u, tb):
                m = unit_no(b, h, tb)
                pe.wait_ge(S["dup_done"], rot_no(b, h) + 1)
                for i, (dst, k0, k1) in enumerate(((psT0, 2, 4), (psT1[0:HD, :], 4, 5))):
                    pe.wait_ge(S["t_ev"], 1 + m * 3 + i + 1)
                    kA, kB = [tile[:, u, tb, j, k0:k1, :].rearrange("p k c -> p (k c)") for j in range(2)]
                    d = diag[:, tb, :, :].rearrange("p j c -> p (j c)")
                    pe.matmul(dst[:, 0:3 * P], kA, d[:, 0:3 * P], start=True, stop=False)
                    pe.matmul(dst[:, P:3 * P], kB, d[:, 3 * P:5 * P], start=False, stop=True)
                    pe.matmul(dst[:, 3 * P:4 * P], kB, d[:, 5 * P:6 * P], start=True, stop=True
                              ).then_inc(S["t_done"], 1)

            def scores(b, h, u, s):
                m = unit_no(b, h, s)
                g, w = s % 2, (s + 1) * P
                pe.wait_ge(S["t_ev"], 1 + m * 3 + 3)
                pe.wait_ge(S["kl_ev"], 1 + m + 1)
                pe.wait_ge(S["mq_done"], rot_no(b, h) + 1)
                pe.wait_ge(S["exp_done"], 1 + step_no(b, h, s) * 2)
                rows = slice(s * P, (s + 1) * P)
                for e in range(2):
                    o = psS[2 * g + e]
                    for j in range(3):
                        q, n = qT[:, 3 * e + j, rows], e + j
                        pe.matmul(o[:, 0:w], q, kT[:, u, n, 0:w], start=(j == 0), stop=False)
                        pe.matmul(o[:, 0:w], q[0:HD, :], klT[0:HD, u, n, 0:w], start=False, stop=False)
                    pe.matmul(o[:, 0:w], mq[0:HD + 1, u, e, rows], mkq[0:HD + 1, 0, 0:w], start=False, stop=False)
                    mm = pe.matmul(o[:, s * P:w], identbig[:, :], causal[:, :], start=False, stop=True)
                mm.then_inc(S["scores_done"], 1)

            def prob_rows(b, h, u, ib):
                pe.wait_ge(S["acc_done"], 3 + step_no(b, h, ib) * 2 + 2)
                pe.wait_ge(S["pt_ev"], 1 + pt_no(b, h, ib))
                for jb in range(ib + 1):
                    mm = pe.transpose(psPT[:, jb * P:(jb + 1) * P], acc[ib % 2][:, jb * P:(jb + 1) * P], ident[:, :])
                mm.then_inc(S["pt_done"], 1)

            def values(b, hp):
                pe.wait_ge(S["pt_ev"], 1 + b * PTS_PER_B + hp * 8 + 2)
                pe.wait_ge(S["vb_done"], 1 + b * PAIRS + hp)
                pe.wait_ge(S["y_ev"], 1 + b * (PAIRS + 1) + hp)
                for jb in range(TB):
                    for u in range(2):
                        mm = pe.matmul(psY[u * HD:(u + 1) * HD, jb * P:T], v_b[:, jb, :], accT[u][:, jb, jb * P:T],
                                       start=(jb == 0), stop=(jb == TB - 1))
                mm.then_inc(S["pv_done"], 1)

            with pe.Fori(0, B) as b:
                norm_rows(b * 2)
                pe.wait_ge(S["h_ready"], b * 2 + 1)
                for tb in range(TB):
                    mm = pe.matmul(bank[3][:, tb * 64:(tb + 1) * 64], hT[:, tb * P:(tb + 1) * P], w_r[:, :],
                                   start=True, stop=True)
                mm.then_inc(S["lg_mm"], 1)
                for tb in range(TB):
                    if tb >= 2:
                        pe.wait_ge(S["qkv_ev"], (b * TB + tb - 1) * 3)
                    for j, i in enumerate((0, 1, 2) if tb % 2 == 0 else (4, 5, 7)):
                        mm = pe.matmul(bank[i][:, :], hT[:, tb * P:(tb + 1) * P], w_qkv[:, j * 512:(j + 1) * 512],
                                       start=True, stop=True)
                    mm.then_inc(S["proj_mm"], 1)
                    if tb == 0:
                        pe.wait_ge(S["mem16"], b + 1)
                        for to in range(TB):
                            for ti in range(to + 1):
                                mm = pe.matmul(psPT[:, to * 64:(to + 1) * 64], before[:, :] if ti == to else ones16[:, :],
                                               member16[:, ti, :, :].rearrange("p h n -> p (h n)"),
                                               start=(ti == 0), stop=(ti == to))
                        mm.then_inc(S["pos_mm"], 1)
                pe.wait_ge(S["sel_cp"], (b + 1) * 4)
                pe.wait_ge(S["qkv_ev"], (b + 1) * TB * 3)
                pe.sem_inc(S["pe_passed"], 1)
                for tb in range(TB):
                    for dst, o, src in ((psT16[0], 0, member16[:, tb, :, :].rearrange("p h n -> p (h n)")),
                                        (psT16[0], T, sel16[:, 0, tb, :]), (psT16[1], 0, sel16[:, 1, tb, :])):
                        mm = pe.transpose(dst[0:HD, o + tb * P:o + (tb + 1) * P], src, ident16[:, :])
                mm.then_inc(S["mk_t"], 1)
                pe.wait_ge(S["mk_ev"], (b + 1) * 2)
                for tb in range(2):
                    sort_q(b, 0, 0, tb)
                    sort_k(b, 0, 0, tb)
                with pe.Fori(0, PAIRS) as hp:
                    for u in range(2):
                        h = hp * 2 + u
                        for s in range(TB):
                            uh, uu, tb = unit_at(h, u, s)
                            scores(b, h, u, s)
                            sort_q(b, uh, uu, tb)
                            if u == 0 and s == 2:
                                values(b, hp)
                            prob_rows(b, *rows_at(h, u, s))
                            sort_k(b, uh, uu, tb)
                prob_rows(b, H - 1, 1, 2)
                prob_rows(b, H - 1, 1, 3)
                values(b, PAIRS)
                pe.wait_ge(S["y_ev"], 1 + (b + 1) * (PAIRS + 1))
                for i in range(PAIRS):
                    mm = pe.matmul(psPT[:, :], w_o[:, i, :], yT[:, i + 1, :], start=(i == 0), stop=(i == PAIRS - 1))
                mm.then_inc(S["wo_mm"], 1)
                pe.wait_ge(S["att_ev"], b + 1)
                for tb in range(TB):
                    mm = pe.transpose(psY[:, tb * P:(tb + 1) * P], att[:, tb * P:(tb + 1) * P], ident[:, :])
                mm.then_inc(S["att_t"], 1)
                norm_rows(b * 2 + 1)
                pe.wait_ge(S["h_ready"], b * 2 + 2)
                for tb in range(TB):
                    mm = pe.matmul(psT0[:, tb * E:(tb + 1) * E], hT[:, tb * P:(tb + 1) * P], w_rt[:, :],
                                   start=True, stop=True)
                mm.then_inc(S["r_mm"], 1)
            pe.wait_ge(S["h2_copy"], B)
            pe.wait_ge(S["r_cev"], B)
            for t_ in range(B):
                for tb in range(TB):
                    mm = pe.transpose(bank[4 + t_][0:E, tb * P:(tb + 1) * P], ecoef[:, t_ * TB + tb, :], ident[:, :])
                mm.then_inc(S["r_cT"], 1)

            def ffn(m, slot_, shared, w_count):
                n0 = m * 16
                w = w_e[slot_]
                pe.wait_ge(S[f"w_slot{slot_}"], w_count)

                def gate_up(i):
                    t_, c_ = i // 4, i % 4
                    if not (shared and i < 2):
                        pe.wait_ge(S["silu_done"], n0 + i - 1)
                        pe.wait_ge(S["hid_done"], n0 + i)
                    rhs = h2T[:, t_ * 512:(t_ + 1) * 512]
                    pe.matmul(bank[i % 2][:, :], w[:, 1, c_ * P:(c_ + 1) * P], rhs, start=True, stop=True)
                    pe.matmul(bank[2 + i % 2][:, :], w[:, 0, c_ * P:(c_ + 1) * P], rhs, start=True, stop=True
                              ).then_inc(S["gu_mm"], 1)

                def down(i):
                    t_, c_ = i // 4, i % 4
                    o = t_ % 2
                    if c_ == 0:
                        if not (shared and t_ < 2):
                            pe.wait_ge(S["ffn_acc"], m * 4 + t_ - 1)
                        if not shared:
                            pe.wait_ge(S["crow_done"], m)
                            pe.matmul(bank[6 + o][:, :], ones8[:, :], crow[:, t_ * 512:(t_ + 1) * 512],
                                      start=True, stop=True).then_inc(S["bc_mm"], 1)
                    pe.wait_ge(S["hid_done"], n0 + i + 2)
                    mm = pe.matmul(bank[4 + o][:, :], w[:, 2, c_ * P:(c_ + 1) * P], hidden[i % 2][:, :],
                                   start=(c_ == 0), stop=(c_ == 3))
                    mm.then_inc(S["hid_used"], 1)
                    if c_ == 3:
                        pe.wait_ge(S["hid_used"], n0 + i + 1)
                        pe.sem_inc(S["down_mm"], 1)

                gate_up(0)
                for i in range(1, 17):
                    if i < 16:
                        gate_up(i)
                    down(i - 1)

            ffn(0, 0, True, 48)
            ffn(1, 1, False, 48)
            with pe.Fori(0, 3) as r:
                ffn(r * 2 + 2, 0, False, r * 48 + 96)
                ffn(r * 2 + 3, 1, False, r * 48 + 96)
            for b in range(B):
                pe.wait_ge(S["fin_g"], b + 1)
                if b >= 2:
                    pe.wait_ge(S["fin_done"], b - 1)
                for tb in range(TB):
                    mm = pe.transpose(bank[b % 2][:, tb * P:(tb + 1) * P],
                                      ffnT[:, b * T + tb * P:b * T + (tb + 1) * P], ident[:, :])
                mm.then_inc(S["fin_t"], 1)


_INS = ['L0_attn_x', 'L0_attn_wq', 'L0_attn_wk', 'L0_attn_wv', 'L0_attn_wr', 'L0_attn_wo', 'L0_ffn_w_router',
        'L0_ffn_w_up', 'L0_ffn_w_gate', 'L0_ffn_w_down', 'L0_ffn_ws_up', 'L0_ffn_ws_gate', 'L0_ffn_ws_down',
        'L0_c', 'L0_wmod']
_OUTS = [((B, T, DIM), 'float32')]


def _rotary_frequencies():
    e = np.arange(0, HD, 2, dtype=np.float32) / np.float32(HD)
    f = np.float32(1.0) / np.power(np.float32(10000.0), e, dtype=np.float32)
    return np.ascontiguousarray(np.broadcast_to(f.astype(np.float32), (P, HALF)))


def kernel(**inputs):
    import numpy as _np
    import concourse.bacc as _bacc
    from concourse import mybir as _mybir
    from concourse.bass_utils import run_bass_kernel_spmd as _run

    nc = _bacc.Bacc("TRN2", target_bir_lowering=False, num_devices=1)
    arrays, args = {}, []
    for name in _INS:
        a = _np.ascontiguousarray(inputs[name])
        arrays[f"in_{name}_dram"] = a
        args.append(nc.dram_tensor(f"in_{name}_dram", a.shape, _mybir.dt.from_np(a.dtype), kind="ExternalInput").ap())
    f = _rotary_frequencies()
    arrays["rotary_frequencies_dram"] = f
    args.append(nc.dram_tensor("rotary_frequencies_dram", f.shape, _mybir.dt.from_np(f.dtype), kind="ExternalInput").ap())
    for i, (shape, dtype) in enumerate(_OUTS):
        dt = _mybir.dt.from_np(_np.dtype(dtype))
        args.append(nc.dram_tensor(f"out_{i}_dram", shape, dt, kind="ExternalOutput").ap())
    block_kernel(nc, *args)
    r = _run(nc, [arrays], core_ids=[0])
    got = tuple(r.results[0][f"out_{i}_dram"] for i in range(len(_OUTS)))
    return got[0]
```

```python
from contextlib import ExitStack

import concourse.bass as bass
from concourse import mybir
import numpy as np

F32 = mybir.dt.float32
F16 = mybir.dt.float16
U32 = mybir.dt.uint32
ALU = mybir.AluOpType
ACT = mybir.ActivationFunctionType
AX_X = mybir.AxisListType.X

P = 128
B, T, DIM = 4, 512, 128
H, KV, HD, NODES = 16, 4, 64, 4
TB = T // P
HP = H + 1
PAIRS = H // 2
HALF = HD // 2
E, HID = 8, 512
BLOCKS = 6
UNITS_PER_B = 4 * H + 2
QKV = (H + 2 * KV) * HD
K0, V0 = H * HD, (H + KV) * HD
BIG = 32768.0
MAGIC = 12582912.0
TWO_PI_HI = 6.28125
TWO_PI_LO = 0.0019353071795864769
PI_CLAMP = 3.1415925
EPS = 1e-5
PTS_PER_B = 4 * H + 2


def block_kernel(nc, x, wq, wk, wv, wr, wo, w_router, w_up, w_gate, w_down, ws_up, ws_gate, ws_down,
                 c, wmod, inv_freq, out):
    ctx = ExitStack()
    with ctx:
        def sb(name, shape, dt=F32):
            return ctx.enter_context(nc.sbuf_tensor(name, shape, dt))

        def sem(name):
            return ctx.enter_context(nc.semaphore(name))

        ctx.enter_context(nc.allow_non_contiguous_dma(reason="small transposed loads"))
        psum = ctx.enter_context(nc.psum_tensor("psum", [P, 8, 512], F32))
        bank = [psum[:, i, :] for i in range(8)]
        psS = bank[0:4]
        psT0, psT1, psPT, psY = bank[4], bank[5], bank[6], bank[7]
        psT16 = [t_[:, :].bitcast(F16) for t_ in (psT0, psT1)]

        ident = sb("ident", [P, P])
        ident16 = sb("ident16", [P, P], F16)
        identbig = sb("identbig", [P, P], F16)
        causal = sb("causal", [P, P], F16)
        before = sb("before", [P, P], F16)
        ones16 = sb("ones16", [P, P], F16)
        headsel = sb("headsel", [P, HP])
        row64 = sb("row64", [P, 1])
        ones8 = sb("ones8", [E, P])
        half_pi = sb("half_pi", [P, 1])
        freq = sb("freq", [P, HALF])
        rank8 = sb("rank8", [P, E])

        w_qkv = sb("w_qkv", [P, QKV])
        w_r = sb("w_r", [P, H * NODES])
        w_o = sb("w_o", [P, PAIRS, DIM])
        w_rt = sb("w_rt", [P, E])

        c_t = sb("c_t", [P, B])
        c_e = sb("c_e", [P, B])
        c_s = sb("c_s", [P, B])
        mod = sb("mod", [P, 6, B])
        gsign = sb("gsign", [P, 2, B])
        gmag = sb("gmag", [P, 2, B])

        xb = sb("xb", [P, TB, DIM])
        stats = sb("stats", [P, TB, 6])
        mv = sb("mv", [P, TB, 2])
        ve = sb("ve", [P, TB])
        sd = sb("sd", [P, TB])
        rs = sb("rs", [P, 3, TB])
        xn = sb("xn", [P, TB, DIM])
        hT = sb("hT", [P, T])
        qkv = sb("qkv", [P, TB, QKV])
        lg = sb("lg", [P, TB, H, NODES])
        lmax = sb("lmax", [P, 2, TB * H])
        ew = sb("ew", [P, TB, H, NODES])
        member = sb("member", [P, TB, H, NODES])
        member16 = sb("member16", [P, TB, H, NODES], F16)
        sel = sb("sel", [P, TB, HP, 2, NODES])
        sel16 = sb("sel16", [P, 2, TB, H * NODES], F16)
        pairs = sb("pairs", [P, TB, HP, BLOCKS, 2], F16)
        prod = sb("prod", [P, TB * H, 2, NODES])
        es = sb("es", [P, TB * H, 2])
        wslot = sb("wslot", [P, TB, H, 2])
        slot = sb("slot", [P, TB * H, 2])
        cosn = sb("cosn", [P, TB, HP, 2, HALF])
        sinn = sb("sinn", [P, TB, HP, 2, HALF])

        pc = [sb(f"pc{s}", [P, TB, 2, HD]) for s in range(2)]
        ps = [sb(f"ps{s}", [P, TB, 2, HD]) for s in range(2)]
        gt, sc = [ps[i][:, :, :, :].rearrange("p t j d -> p (t j d)")[:, 0:6 * TB * H].rearrange(
            "p (k a) -> p k a", k=6) for i in range(2)]
        rot = pc
        sizes = [BLOCKS * T, 2 * NODES * T, 2 * NODES * T, 2 * TB * 2 * 5 * HD, TB * BLOCKS * P]
        ends = [sum(sizes[:i]) for i in range(len(sizes) + 1)]
        work = sb("work", [P, ends[-1]], F16)
        part = [work[:, ends[i]:ends[i + 1]] for i in range(len(sizes))]
        qT = part[0].rearrange("p (j t) -> p j t", j=BLOCKS)
        kT = part[1].rearrange("p (u n t) -> p u n t", u=2, n=NODES)
        klT = part[2].rearrange("p (u n t) -> p u n t", u=2, n=NODES)
        tile = part[3].rearrange("p (u t s k c) -> p u t s k c", u=2, t=TB, s=2, k=5)
        diag = part[4].rearrange("p (t j c) -> p t j c", t=TB, j=BLOCKS)
        mkq = sb("mkq", [P, 3, T], F16)
        mq = sb("mq", [P, 2, 2, T], F16)

        negmax = [sb(f"negmax{g}", [P, 2]) for g in range(2)]
        probs = [sb(f"probs{g}", [P, 2, T]) for g in range(2)]
        den = [sb(f"den{g}", [P, 2]) for g in range(2)]
        rden = [sb(f"rden{g}", [P, 2]) for g in range(2)]
        coef = [sb(f"coef{g}", [P, 2]) for g in range(2)]
        acc = [sb(f"acc{g}", [P, T]) for g in range(2)]
        accT_all = sb("accT", [P, 2, TB, T])
        accT = [accT_all[:, u, :, :] for u in range(2)]
        v_b = sb("v_b", [P, TB, HD])
        yT = sb("yT", [P, PAIRS + 1, T])

        chunks = [(0, 1), (1, 3), (3, 5), (5, PAIRS)]
        RED = int(np.sum(_rotary_frequencies()[0] * (T - 1) >= 3.14))
        ang_flat = accT_all[:, :, :, :].rearrange("p u j t -> p (u j t)")
        red_flat = yT[:, :, :].rearrange("p c t -> p (c t)")
        ang = [ang_flat[:, p0 * 4 * TB * HALF:p1 * 4 * TB * HALF].rearrange("p (t a f) -> p t a f", t=TB, f=HALF)
               for p0, p1 in chunks]
        red = [red_flat[:, 0:(p1 - p0) * 4 * TB * RED].rearrange("p (a f) -> p a f", f=RED) for p0, p1 in chunks]

        x1 = sb("x1", [P, B * TB, DIM])
        h2 = sb("h2", [P, 2, B * T], F16)
        rl = sb("rl", [P, TB, E])
        rr = sb("rr", [P, 4, TB, E])
        rm = sb("rm", [P, 4, TB])
        ecoef = sb("ecoef", [P, B * TB, E])
        att = xn[:, :, :].rearrange("p t d -> p (t d)")
        w_mod = probs[0][:, :, :].rearrange("p e t -> p (e t)")[:, 0:6 * DIM]
        w_e = [qkv[:, i, :].rearrange("p (k n) -> p k n", k=3) for i in range(2)]
        w_hl = [qkv[:, 2 + i, :].bitcast(F16).rearrange("p (l k n) -> p l k n", l=2, k=3) for i in range(2)]
        cos_flat = cosn[:, :, :, :, :].rearrange("p t h s f -> p (t h s f)")
        sin_flat = sinn[:, :, :, :, :].rearrange("p t h s f -> p (t h s f)")
        ffnT = cos_flat[:, 0:B * T]
        crow = cos_flat[0:E, B * T:2 * B * T]
        coefT = sin_flat[0:E, 0:B * T]
        hidden = [sin_flat[:, 2048 + 512 * i:2560 + 512 * i] for i in range(2)]
        hid16 = [work[:, 1024 * i:1024 * (i + 1)].rearrange("p (l n) -> p l n", l=2) for i in range(2)]
        gateb = [sin_flat[:, 3072 + 512 * i:3584 + 512 * i] for i in range(2)]
        bc = [ps[i][:, :, :, :].rearrange("p t j d -> p (t j d)") for i in range(2)]
        wtd = [pc[i][:, :, :, :].rearrange("p t j d -> p (t j d)") for i in range(2)]

        names = """loaded x_in w_slot0 w_slot1 out_done const_done ident_done init_done c_exp c_sum c_rec
            c_silu mod_mm mod_raw mod_sign mod_mag mod_done bn_s bn_a var_e std_dev rs_0 rs_1 rs_2
            rs_3 xn_done xn_t h_ready proj_mm qkv_ev lg_mm rank_g rank_s rank_m l_max l_sub l_exp
            l_mem l_rec w_done mem16 pos_mm slots_w ang_mul ang_k ang_n ang_r1 ang_r2 ang_clamp
            ang_abs trig_sin trig_cos pc_done ps_done rot_done hi_done lo_done dup_done diag_done
            mq_done sel_a sel_b sel_cp pr_w es_done es_sum pe_passed mk_t mk_ev row_done head_sel
            pr_pos t_done t_ev kl_ev scores_done negmax_done exp_done rden_done coef_done acc_done
            pt_done pt_ev pv_done y_ev vb_done wo_mm att_ev att_t x1_done x1_kept passed r_mm r_ev
            r_max r_sub r_exp r_eq r_rk r_rm r_sum r_rec r_c r_cT r_cTev r_cev h2_copy h2_low
            pool_passed w_hi w_lo hid_hi hid_lo crow_done bc_mm bc_ev gu_mm silu_done hid_done
            down_mm wtd_done ffn_acc hid_used fin_g fin_t fin_done""".split()
        S = {n: sem(n) for n in names}

        kv_of = lambda h: K0 + (h // (H // KV)) * HD

        def step_no(b, h, s):
            return b * (4 * H) + h * 4 + s

        def rot_no(b, h):
            return b * HP + h

        def pt_no(b, h, ib):
            return b * PTS_PER_B + 2 + h * 4 + ib

        def unit_no(b, h, tb):
            return b * UNITS_PER_B + h * 4 + tb

        def unit_at(h, u, s):
            return (h, u, s + 2) if s < 2 else (h + 1, 1 - u, s - 2)

        def rows_at(h, u, s):
            return (h - 1, 1 - u, s + 2) if s < 2 else (h, u, s - 2)

        block = ctx.enter_context(nc.Block())

        @block.sync
        def _(sp):
            n_small = 0
            for dst, src in ((freq[:, :], inv_freq), (c_t[:, :], c.rearrange("b d -> d b")),
                             (w_mod[:, :], wmod), (w_qkv[:, 0:K0], wq), (w_qkv[:, K0:V0], wk),
                             (w_qkv[:, V0:QKV], wv), (w_r[:, :], wr),
                             (w_o[:, :, :], wo.rearrange("(c p) n -> p c n", p=P)), (w_rt[:, :], w_router)):
                sp.dma_start(dst, src).then_inc(S["loaded"], 16)
                n_small += 1
            with sp.Fori(0, B) as b:
                sp.wait_ge(S["x1_kept"], 1 + b)
                sp.dma_start(xb[:, :, :], x[bass.ds(b, 1), :, :].rearrange("a (t p) d -> p (a t) d", p=P)
                             ).then_inc(S["x_in"], 16)

        def load_expert(eng, i, up, gate, down):
            eng.dma_start(w_e[i][:, 0, :], up).then_inc(S[f"w_slot{i}"], 16)
            eng.dma_start(w_e[i][:, 1, :], gate).then_inc(S[f"w_slot{i}"], 16)
            eng.dma_start(w_e[i][:, 2, :].rearrange("p (c n) -> p c n", c=4),
                          down.rearrange("(c p) n -> p c n", p=P)).then_inc(S[f"w_slot{i}"], 16)

        @block.sync
        def _(sp):
            sp.wait_ge(S["wo_mm"], B)
            load_expert(sp, 0, ws_up, ws_gate, ws_down)
            load_expert(sp, 1, w_up[0], w_gate[0], w_down[0])
            with sp.Fori(0, 3) as r:
                for i in range(2):
                    e = r * 2 + 1 + i
                    sp.wait_ge(S["w_lo"], r * 2 + 1 + i)
                    load_expert(sp, i, w_up[bass.ds(e, 1)].rearrange("a p n -> (a p) n"),
                                w_gate[bass.ds(e, 1)].rearrange("a p n -> (a p) n"),
                                w_down[bass.ds(e, 1)].rearrange("a p n -> (a p) n"))
            for b in range(B):
                sp.wait_ge(S["fin_done"], b + 1)
                sp.dma_start(out[b].rearrange("(t p) d -> p t d", p=P),
                             x1[:, b * TB:(b + 1) * TB, :]).then_inc(S["out_done"], 16)
            sp.wait_ge(S["out_done"], 16 * B)

        @block.gpsimd
        def _(pool):
            for t_, v in ((ident, 0.0), (ident16, 0.0), (identbig, 0.0), (causal, 0.0), (before, 1.0),
                          (ones16, 1.0), (headsel, 1.0), (row64, 0.0), (ones8, 1.0),
                          (half_pi, float(np.pi / 2))):
                pool.memset(t_[:, :], v).then_inc(S["const_done"], 1)
            pool.iota(rank8[:, :], [[-1, E]], base=E, channel_multiplier=0,
                      allow_small_or_imprecise_dtypes=True).then_inc(S["const_done"], 1)
            for u in range(2):
                pool.memset(acc[u][:, :], 0.0).then_inc(S["init_done"], 1)
                pool.memset(accT[u][:, :, :], 0.0).then_inc(S["init_done"], 1)
            pool.memset(mkq[:, 0, :], BIG).then_inc(S["init_done"], 1)
            pool.memset(mkq[:, 1:3, :], -BIG).then_inc(S["init_done"], 1)
            pool.memset(v_b[:, :, :], 0.0).then_inc(S["init_done"], 1)
            pool.memset(cosn[:, :, H, :, :], 0.0).then_inc(S["init_done"], 1)
            pool.memset(sinn[:, :, H, :, :], 0.0).then_inc(S["init_done"], 1)
            pool.memset(sel[:, :, :, :, :], 0.0).then_inc(S["init_done"], 1)
            pool.memset(pairs[:, :, :, :, :], 0.0).then_inc(S["init_done"], 1)
            pool.wait_ge(S["const_done"], 11)
            for t_, v in ((ident, 1.0), (ident16, 1.0), (identbig, BIG)):
                pool.affine_select(out=t_[:, :], in_=t_[:, :], compare_op=ALU.not_equal, fill=v, base=0,
                                   pattern=[[-1, P]], channel_multiplier=1).then_inc(S["ident_done"], 1)
            pool.affine_select(out=row64[:, :], in_=row64[:, :], compare_op=ALU.not_equal, fill=1.0, base=-HD,
                               pattern=[[0, 1]], channel_multiplier=1).then_inc(S["ident_done"], 1)
            pool.affine_select(out=headsel[:, :], in_=headsel[:, :], compare_op=ALU.is_ge, fill=0.0, base=0,
                               pattern=[[-NODES, HP]], channel_multiplier=1).then_inc(S["row_done"], 1)
            pool.affine_select(out=causal[:, :], in_=causal[:, :], compare_op=ALU.is_ge, fill=-BIG, base=0,
                               pattern=[[-1, P]], channel_multiplier=1).then_inc(S["ident_done"], 1)
            pool.affine_select(out=before[:, :], in_=before[:, :], compare_op=ALU.is_gt, fill=0.0, base=0,
                               pattern=[[1, P]], channel_multiplier=-1).then_inc(S["ident_done"], 1)

            pool.wait_ge(S["row_done"], 1)
            pool.affine_select(out=headsel[:, :], in_=headsel[:, :], compare_op=ALU.is_ge, fill=0.0,
                               base=NODES - 1, pattern=[[NODES, HP]], channel_multiplier=-1
                               ).then_inc(S["ident_done"], 1)

            pool.sem_inc(S["lo_done"], 1)

            def half_views(s, j):
                return [v[s][:, :, j, :].rearrange("p t (a f) -> p t a f", a=2) for v in (pc, ps)]

            def rotate_head(b, h, u, pair):
                r = rot_no(b, h)
                pool.wait_ge(S["trig_cos"], b * PAIRS + pair + 1)
                pool.wait_ge(S["qkv_ev"], (b + 1) * TB * 3)
                pool.wait_ge(S["hi_done"], 1 + r * 2)
                pool.wait_ge(S["lo_done"], 1 + r * 2)
                for s in range(2):
                    cs, sn = [v[:, :, bass.ds(h, 1), s, :] for v in (cosn, sinn)]
                    for j, col in ((0, h * HD), (1, kv_of(h))):
                        src = qkv[:, :, bass.ds(col, HD)].rearrange("p t (a f) -> p t a f", a=2)
                        pool.tensor_tensor(half_views(s, j)[0], src, cs.to_broadcast([P, TB, 2, HALF]), ALU.mult
                                           ).then_inc(S["pc_done"], 1)
                        for half in range(2):
                            pool.tensor_tensor(ps[s][:, :, j, half * HALF:(half + 1) * HALF],
                                               qkv[:, :, bass.ds(col + (1 - half) * HALF, HALF)],
                                               sn.rearrange("p t a f -> p t (a f)"), ALU.mult
                                               ).then_inc(S["ps_done"], 1)
                for s in range(2):
                    pool.wait_ge(S["pc_done"], r * 4 + s * 2 + 2)
                    pool.wait_ge(S["ps_done"], r * 8 + s * 4 + 4)
                    for half, op in ((0, ALU.subtract), (1, ALU.add)):
                        sl = slice(half * HALF, (half + 1) * HALF)
                        pool.tensor_tensor(rot[s][:, :, :, sl], pc[s][:, :, :, sl], ps[s][:, :, :, sl], op
                                           ).then_inc(S["rot_done"], 1)
                pool.wait_ge(S["rot_done"], r * 4 + 4)
                for s in range(2):
                    pool.wait_ge(S["hi_done"], 1 + r * 2 + s + 1)
                    pool.tensor_tensor(tile[:, u, :, s, 1:5:3, :], rot[s][:, :, :, :], tile[:, u, :, s, 0:3:2, :],
                                       ALU.subtract).then_inc(S["lo_done"], 1)

            with pool.Fori(0, B) as b:
                with pool.Fori(0, PAIRS) as hp:
                    for u in range(2):
                        rotate_head(b, hp * 2 + u, u, hp)
                rotate_head(b, H, 0, PAIRS - 1)

            def split_weights(m, i, w_count):
                pool.wait_ge(S[f"w_slot{i}"], w_count)
                if not (isinstance(m, int) and m < 2):
                    pool.wait_ge(S["down_mm"], (m - 1) * 4)
                pool.sem_inc(S["pool_passed"], 1)
                hi, lo = [w_hl[i][:, l, :, :].rearrange("p k n -> p (k n)") for l in range(2)]
                w = w_e[i].rearrange("p k n -> p (k n)")
                pool.tensor_copy(hi, w).then_inc(S["w_hi"], 1)
                pool.wait_ge(S["w_hi"], m + 1)
                pool.tensor_tensor(lo, w, hi, ALU.subtract).then_inc(S["w_lo"], 1)

            for m in range(2):
                split_weights(m, m, 48)
            with pool.Fori(0, 3) as r:
                for i in range(2):
                    split_weights(r * 2 + 2 + i, i, r * 48 + 96)

        @block.scalar
        def _(act):
            act.wait_ge(S["loaded"], 16 * 9)
            act.activation(c_e[:, :], c_t[:, :], ACT.Exp, scale=-1.0).then_inc(S["c_exp"], 1)
            act.sem_inc(S["exp_done"], 4)
            for name in ("t_ev", "pt_ev", "y_ev", "vb_done"):
                act.sem_inc(S[name], 1)

            def norm_and_project(b, turn, which):
                act.wait_ge(S["var_e"], turn + 1)
                act.activation(sd[:, :], ve[:, :], ACT.Sqrt).then_inc(S["std_dev"], 1)
                act.wait_ge(S["xn_t"], turn + 1)
                act.wait_ge(S["mod_done"], 3)
                act.activation(hT[:, :], psPT[:, :], ACT.Identity,
                               bias=mod[:, which, bass.ds(b, 1)], scale=mod[:, which + 1, bass.ds(b, 1)]
                               ).then_inc(S["h_ready"], 1)

            def move_pt(b, h, u, ib):
                act.wait_ge(S["pt_done"], pt_no(b, h, ib) + 1)
                w = ib + 1
                act.activation(accT[u][:, 0:w, ib * P:(ib + 1) * P],
                               psPT[:, 0:w * P].rearrange("p (j i) -> p j i", j=w), ACT.Copy
                               ).then_inc(S["pt_ev"], 1)

            def keep_q(b, h, tb):
                m, rows = unit_no(b, h, tb), slice(tb * P, (tb + 1) * P)
                for j, bank_ in enumerate((psT0, psT1)):
                    act.wait_ge(S["t_done"], m * 4 + j + 1)
                    act.activation(qT[:, 3 * j:3 * j + 3, rows], bank_[:, 0:3 * P].rearrange("p (j t) -> p j t", j=3),
                                   ACT.Copy).then_inc(S["t_ev"], 1)

            def keep_k(b, h, u, tb):
                m = unit_no(b, h, tb)
                act.wait_ge(S["t_done"], m * 4 + 3)
                act.activation(kT[:, u, :, tb * P:(tb + 1) * P], psT0[:, :].rearrange("p (n t) -> p n t", n=NODES),
                               ACT.Copy).then_inc(S["t_ev"], 1)

            with act.Fori(0, B) as b:
                norm_and_project(b, b * 2, 0)
                def trigonometry(i):
                    p0, p1 = chunks[i]
                    heads = slice(2 * p0, 2 * p1)
                    a_ = ang[i].rearrange("p t a f -> p t (a f)")
                    act.wait_ge(S["ang_clamp"], b * len(chunks) + i + 1)
                    act.activation(sinn[:, :, heads, :, :].rearrange("p t h s f -> p t (h s f)"), a_, ACT.Sin
                                   ).then_inc(S["trig_sin"], 1)
                    act.activation(a_, a_, ACT.Abs).then_inc(S["ang_abs"], 1)
                    act.wait_ge(S["ang_abs"], b * len(chunks) + i + 1)
                    act.activation(cosn[:, :, heads, :, :].rearrange("p t h s f -> p t (h s f)"), a_, ACT.Sin,
                                   scale=-1.0, bias=half_pi[:, 0:1]).then_inc(S["trig_cos"], p1 - p0)

                for tb in range(TB):
                    act.wait_ge(S["proj_mm"], b * TB + tb + 1)
                    for j, i in enumerate((0, 1, 2) if tb % 2 == 0 else (4, 5, 7)):
                        act.activation(qkv[:, tb, j * 512:(j + 1) * 512], bank[i][:, :], ACT.Copy,
                                       scale=HD ** -0.5 if j < 2 else 1.0).then_inc(S["qkv_ev"], 1)
                    if tb == 1:
                        act.wait_ge(S["l_sub"], b + 1)
                        act.activation(ew[:, :, :, :], ew[:, :, :, :], ACT.Exp).then_inc(S["l_exp"], 1)
                        act.preload_act_table(ACT.Sin)
                        trigonometry(0)

                for i in range(1, len(chunks) - 1):
                    trigonometry(i)
                act.wait_ge(S["mk_t"], b + 1)
                act.activation(mkq[0:HD, 0:2, :].rearrange("p k t -> p (k t)"), psT16[0][0:HD, :], ACT.Copy,
                               scale=BIG).then_inc(S["mk_ev"], 1)
                act.activation(mkq[0:HD, 2, :], psT16[1][0:HD, 0:T], ACT.Copy, scale=BIG).then_inc(S["mk_ev"], 1)
                trigonometry(len(chunks) - 1)
                act.preload_act_table(ACT.Exp)
                for tb in range(2):
                    keep_q(b, 0, tb)
                    keep_k(b, 0, 0, tb)
                with act.Fori(0, PAIRS // 2) as hq:
                    for v in range(4):
                        hp, u, h = hq * 2 + v // 2, v % 2, hq * 4 + v
                        for s in range(TB):
                            w, g = (s + 1) * P, s % 2
                            k = step_no(b, h, s)
                            uh, uu, tb = unit_at(h, u, s)
                            keep_q(b, uh, tb)
                            move_pt(b, *rows_at(h, u, s))
                            keep_k(b, uh, uu, tb)
                            act.wait_ge(S["acc_done"], 1 + k * 2)
                            for e in range(2):
                                act.wait_ge(S["negmax_done"], k * 2 + e + 1)
                                act.activation(probs[g][:, e, 0:w], psS[2 * g + e][:, 0:w], ACT.Exp,
                                               bias=negmax[g][:, e:e + 1], accum_out=den[g][:, e:e + 1]
                                               ).then_inc(S["exp_done"], 1)
                            if u == 0 and s == 2:
                                act.wait_ge(S["pv_done"], b * (PAIRS + 1) + hp + 1)
                                act.activation(yT[:, bass.ds(hp, 1), :].rearrange("p a t -> p (a t)"),
                                               psY[:, :], ACT.Copy).then_inc(S["y_ev"], 1)
                                act.activation(v_b[:, :, :], qkv[:, :, bass.ds(hq * HD + V0, HD)],
                                               ACT.Copy).then_inc(S["vb_done"], 1)
                move_pt(b, H - 1, 1, 2)
                move_pt(b, H - 1, 1, 3)
                act.wait_ge(S["pv_done"], (b + 1) * (PAIRS + 1))
                act.activation(yT[:, PAIRS, :], psY[:, :], ACT.Copy).then_inc(S["y_ev"], 1)
                act.wait_ge(S["wo_mm"], b + 1)
                act.activation(att[:, :], psPT[:, :], ACT.Copy, scale=mod[:, 2, bass.ds(b, 1)]
                               ).then_inc(S["att_ev"], 1)
                norm_and_project(b, b * 2 + 1, 3)
                act.wait_ge(S["h_ready"], b * 2 + 2)
                act.activation(h2[:, 0, bass.ds(b * T, T)], hT[:, :], ACT.Copy).then_inc(S["h2_copy"], 1)
                act.wait_ge(S["r_sub"], b + 1)
                act.activation(rr[:, 0, :, :], rr[:, 0, :, :], ACT.Exp).then_inc(S["r_exp"], 1)

            def gates(n0):
                for i in range(16):
                    n = n0 + i
                    act.wait_ge(S["gu_mm"], n + 1)
                    act.wait_ge(S["hid_done"], n)
                    act.activation(gateb[i % 2][:, :], bank[i % 2][:, :], ACT.Silu).then_inc(S["silu_done"], 1)
                    high_hidden(n, i % 2)

            def high_hidden(n, i):
                act.wait_ge(S["hid_done"], n + 2)
                if not (isinstance(n, int) and n < 2):
                    act.wait_ge(S["hid_used"], n - 1)
                act.activation(hid16[i][:, 0, :], hidden[i][:, :], ACT.Copy).then_inc(S["hid_hi"], 1)

            gates(0)
            gates(16)
            with act.Fori(0, 3) as r:
                gates(r * 32 + 32)
                gates(r * 32 + 48)
            for b in range(B):
                act.wait_ge(S["ffn_acc"], 32)
                act.activation(ffnT[:, b * T:(b + 1) * T], ffnT[:, b * T:(b + 1) * T], ACT.Copy,
                               scale=mod[:, 5, b:b + 1]).then_inc(S["fin_g"], 1)

        @block.vector
        def _(dve):
            dve.wait_ge(S["c_exp"], 1)
            dve.tensor_scalar(c_e[:, :], c_e[:, :], 1.0, None, ALU.add).then_inc(S["c_sum"], 1)
            dve.wait_ge(S["c_sum"], 1)
            dve.reciprocal(c_s[:, :], c_e[:, :]).then_inc(S["c_rec"], 1)
            dve.wait_ge(S["c_rec"], 1)
            dve.tensor_tensor(c_s[:, :], c_s[:, :], c_t[:, :], ALU.mult).then_inc(S["c_silu"], 1)
            dve.wait_ge(S["mod_mm"], 1)
            dve.tensor_copy(mod[:, :, :].rearrange("p a b -> p (a b)"), psT0[:, 0:6 * B]).then_inc(S["mod_raw"], 1)
            dve.wait_ge(S["mod_raw"], 1)
            for j in range(2):
                dve.tensor_scalar(mod[:, 3 * j + 1, :], mod[:, 3 * j + 1, :], 1.0, None, ALU.add
                                  ).then_inc(S["mod_done"], 1)
            g_raw = mod[:, :, :].rearrange("p (j k) b -> p j k b", j=2)[:, :, 2, :]
            dve.tensor_scalar(gsign[:, :, :], g_raw, 0.0, 2.0, ALU.is_ge, ALU.mult).then_inc(S["mod_sign"], 1)
            dve.scalar_tensor_tensor(gmag[:, :, :], g_raw, -1.0, g_raw, ALU.mult, ALU.max).then_inc(S["mod_sign"], 1)
            dve.wait_ge(S["mod_sign"], 2)
            dve.tensor_scalar(gmag[:, :, :], gmag[:, :, :], 0.25, None, ALU.max).then_inc(S["mod_mag"], 1)
            dve.wait_ge(S["mod_mag"], 1)
            dve.scalar_tensor_tensor(g_raw, gsign[:, :, :], -1.0, gmag[:, :, :], ALU.add, ALU.mult
                                     ).then_inc(S["mod_done"], 1)

            def layer_norm(turn):
                for tb in range(TB):
                    dve.bn_stats(stats[:, tb, :], xb[:, tb, :]).then_inc(S["bn_s"], 1)
                dve.wait_ge(S["bn_s"], (turn + 1) * TB)
                dve.sem_inc(S["passed"], 1)
                for tb in range(TB):
                    dve.bn_aggr(mv[:, tb, :], stats[:, tb, :]).then_inc(S["bn_a"], 1)
                dve.wait_ge(S["bn_a"], (turn + 1) * TB)
                dve.tensor_scalar(ve[:, :], mv[:, :, 1], EPS, None, ALU.add).then_inc(S["var_e"], 1)
                dve.wait_ge(S["std_dev"], turn + 1)
                dve.reciprocal(rs[:, 0, :], sd[:, :]).then_inc(S["rs_0"], 1)
                dve.wait_ge(S["rs_0"], turn + 1)
                dve.tensor_tensor(rs[:, 1, :], rs[:, 0, :], rs[:, 0, :], ALU.mult).then_inc(S["rs_1"], 1)
                dve.wait_ge(S["rs_1"], turn + 1)
                dve.scalar_tensor_tensor(rs[:, 2, :], rs[:, 1, :], -0.5, ve[:, :], ALU.mult, ALU.mult
                                         ).then_inc(S["rs_2"], 1)
                dve.wait_ge(S["rs_2"], turn + 1)
                dve.scalar_tensor_tensor(rs[:, 1, :], rs[:, 2, :], 1.5, rs[:, 0, :], ALU.add, ALU.mult
                                         ).then_inc(S["rs_3"], 1)
                dve.wait_ge(S["rs_3"], turn + 1)
                for tb in range(TB):
                    dve.tensor_scalar(xn[:, tb, :], xb[:, tb, :], mv[:, tb, 0:1], rs[:, 1, tb:tb + 1],
                                      ALU.subtract, ALU.mult).then_inc(S["xn_done"], 1)

            def high(b, h, u):
                r = rot_no(b, h)
                for s in range(2):
                    dve.wait_ge(S["rot_done"], r * 4 + s * 2 + 2)
                    dve.tensor_copy(tile[:, u, :, s, 0:3:2, :], rot[s][:, :, :, :]).then_inc(S["hi_done"], 1)

            def double(b, h, u):
                dve.wait_ge(S["hi_done"], 1 + rot_no(b, h) * 2 + 2)
                dve.tensor_copy(tile[:, u, :, :, 3, :], tile[:, u, :, :, 2, :]).then_inc(S["dup_done"], 1)

            def diagonals(b, h, tb):
                r = rot_no(b, h)
                dve.tensor_tensor(
                    diag[:, tb, :, :].rearrange("p j (c k) -> p j c k", k=2),
                    ident16[:, :].rearrange("p (c k) -> p c k", k=2).unsqueeze(1).to_broadcast([P, BLOCKS, P // 2, 2]),
                    pairs[:, tb, bass.ds(h, 1), :, :].rearrange("p a j k -> p (a j) k").unsqueeze(2).to_broadcast(
                        [P, BLOCKS, P // 2, 2]), ALU.mult).then_inc(S["diag_done"], 1)

            def query_masks(b, h, u):
                dve.tensor_scalar(mq[0:HD + 1, u, :, :], mkq[0:HD + 1, 1:3, :],
                                  headsel[0:HD + 1, bass.ds(h, 1)] if not isinstance(h, int)
                                  else headsel[0:HD + 1, h:h + 1], None, ALU.mult).then_inc(S["mq_done"], 1)

            def keep_kl(b, h, u, tb):
                m = unit_no(b, h, tb)
                dve.wait_ge(S["t_done"], m * 4 + 4)
                dve.tensor_copy(klT[0:HD, u, :, tb * P:(tb + 1) * P],
                                psT1[0:HD, :].rearrange("p (n t) -> p n t", n=NODES)).then_inc(S["kl_ev"], 1)

            def row_max(b, h, s, e):
                g, w = s % 2, (s + 1) * P
                dve.wait_ge(S["scores_done"], step_no(b, h, s) * 2 + e + 1)
                dve.tensor_reduce(negmax[g][:, e:e + 1], psS[2 * g + e][:, 0:w], AX_X, ALU.max, negate=True
                                  ).then_inc(S["negmax_done"], 1)

            def inverse_sums(b, h, s):
                dve.wait_ge(S["exp_done"], 4 + step_no(b, h, s) * 2 + 2)
                dve.reciprocal(rden[s % 2][:, :], den[s % 2][:, :]).then_inc(S["rden_done"], 1)

            def coefficients(b, h, s):
                g = s % 2
                dve.wait_ge(S["rden_done"], step_no(b, h, s) + 1)
                dve.tensor_tensor(coef[g][:, :], rden[g][:, :],
                                  wslot[:, s, bass.ds(h, 1), :].rearrange("p a n -> p (a n)"), ALU.mult
                                  ).then_inc(S["coef_done"], 1)

            def weigh_a(b, h, s):
                k, g, w = step_no(b, h, s), s % 2, (s + 1) * P
                dve.wait_ge(S["coef_done"], k + 1)
                dve.wait_ge(S["pt_done"], pt_no(b, h, s) - 1)
                dve.tensor_scalar(acc[g][:, 0:w], probs[g][:, 0, 0:w], coef[g][:, 0:1], None, ALU.mult
                                  ).then_inc(S["acc_done"], 1)

            def weigh_b(b, h, s):
                k, g, w = step_no(b, h, s), s % 2, (s + 1) * P
                dve.wait_ge(S["acc_done"], 3 + k * 2 + 1)
                dve.scalar_tensor_tensor(acc[g][:, 0:w], probs[g][:, 1, 0:w], coef[g][:, 1:2], acc[g][:, 0:w],
                                         ALU.mult, ALU.add).then_inc(S["acc_done"], 1)

            dve.wait_ge(S["ident_done"], 7)
            dve.tensor_scalar(headsel[:, :], headsel[:, :], row64[:, 0:1], None, ALU.max).then_inc(S["head_sel"], 1)
            dve.wait_ge(S["head_sel"], 1)
            dve.sem_inc(S["kl_ev"], 1)
            dve.sem_inc(S["acc_done"], 3)
            dve.sem_inc(S["hi_done"], 1)
            dve.sem_inc(S["x1_kept"], 1)
            dve.wait_ge(S["ident_done"], 7)
            dve.wait_ge(S["init_done"], 11)
            with dve.Fori(0, B) as b:
                dve.wait_ge(S["x_in"], (b + 1) * 16)
                layer_norm(b * 2)
                dve.wait_ge(S["lg_mm"], b + 1)
                dve.tensor_copy(lg[:, :, :, :].rearrange("p t h n -> p (t h n)"), bank[3][:, 0:TB * H * NODES]
                                ).then_inc(S["rank_g"], 1)
                dve.wait_ge(S["rank_g"], b + 1)
                L = lg[:, :, :, :].rearrange("p t h n -> p (t h) n")
                M = member[:, :, :, :].rearrange("p t h n -> p (t h) n")
                W = ew[:, :, :, :].rearrange("p t h n -> p (t h) n")
                duo = [(0, 1), (0, 2), (0, 3), (1, 2), (1, 3), (2, 3)]
                for i, (m, n) in enumerate(duo):
                    dve.tensor_tensor(gt[:, i, :], L[:, :, m], L[:, :, n], ALU.is_ge).then_inc(S["rank_s"], 1)
                dve.tensor_reduce(lmax[:, 0, :], L, AX_X, ALU.max).then_inc(S["l_max"], 1)
                dve.wait_ge(S["l_max"], b + 1)
                dve.tensor_tensor(W, L, lmax[:, 0, :].unsqueeze(2).to_broadcast([P, TB * H, NODES]), ALU.subtract
                                  ).then_inc(S["l_sub"], 1)
                dve.wait_ge(S["rank_s"], (b + 1) * 6)
                for i, (a, c_, op) in enumerate(((0, 1, ALU.add), (3, 4, ALU.add), (5, 1, ALU.subtract),
                                                 (2, 4, ALU.add))):
                    dve.tensor_tensor(sc[:, i, :], gt[:, a, :], gt[:, c_, :], op).then_inc(S["rank_m"], 1)
                dve.wait_ge(S["rank_m"], b * 8 + 4)
                for i, a, op in ((0, 2, ALU.add), (1, 0, ALU.subtract), (2, 3, ALU.subtract), (3, 5, ALU.add)):
                    dve.tensor_tensor(sc[:, i, :], sc[:, i, :], gt[:, a, :], op).then_inc(S["rank_m"], 1)
                dve.wait_ge(S["rank_m"], b * 8 + 8)
                for n, (v, op) in enumerate(((1.5, ALU.is_gt), (0.5, ALU.is_gt), (-0.5, ALU.is_gt), (1.5, ALU.is_lt))):
                    dve.tensor_scalar(M[:, :, n], sc[:, n, :], v, None, op).then_inc(S["l_mem"], 1)
                dve.wait_ge(S["l_mem"], (b + 1) * 4)
                dve.tensor_copy(member16[:, :, :, :], member[:, :, :, :]).then_inc(S["mem16"], 1)
                sA, sB = sel[:, :, 0:H, 0, :], sel[:, :, 0:H, 1, :]
                Mb = lambda n: member[:, :, :, n]
                dve.tensor_copy(sA[:, :, :, 0], Mb(0)).then_inc(S["sel_a"], 1)
                dve.tensor_tensor(sA[:, :, :, 1], Mb(1), Mb(0), ALU.is_gt).then_inc(S["sel_a"], 1)
                dve.tensor_tensor(sA[:, :, :, 2], Mb(2), Mb(3), ALU.mult).then_inc(S["sel_a"], 1)
                dve.wait_ge(S["sel_a"], (b + 1) * 3)
                dve.tensor_tensor(sB, member[:, :, :, :], sA, ALU.subtract).then_inc(S["sel_b"], 1)
                dve.wait_ge(S["sel_b"], b + 1)
                for i, v in enumerate((sA, sB)):
                    dve.tensor_copy(sel16[:, i, :, :].rearrange("p t (h n) -> p t h n", h=H), v
                                    ).then_inc(S["sel_cp"], 1)
                    dve.tensor_copy(
                        pairs[:, :, :, 3 * i:3 * i + 3, :].rearrange("p t h j k -> p (t h) j k"),
                        sel[:, :, :, i, i:i + 3].rearrange("p t h j -> p (t h) j").unsqueeze(3).to_broadcast(
                            [P, TB * HP, 3, 2])).then_inc(S["sel_cp"], 1)
                dve.wait_ge(S["pos_mm"], b + 1)
                pos = psPT[:, 0:TB * H * NODES].rearrange("p (t h n) -> p t h n", t=TB, h=H)
                PR = prod[:, :, :, :].rearrange("p (t h) i n -> p t h i n", t=TB)
                for i, v in enumerate((sA, sB)):
                    dve.tensor_tensor(PR[:, :, :, i, :], pos, v, ALU.mult).then_inc(S["pr_pos"], 1)
                dve.wait_ge(S["pr_pos"], (b + 1) * 2)
                dve.tensor_reduce(slot[:, :, :], prod[:, :, :, :], AX_X, ALU.add).then_inc(S["slots_w"], 1)
                dve.wait_ge(S["slots_w"], b + 1)

                def angles(i):
                    p0, p1 = chunks[i]
                    n = b * len(chunks) + i + 1
                    c0, c1 = 4 * p0, 4 * p1
                    a_, r_ = ang[i].rearrange("p t a f -> p (t a) f")[:, :, 0:RED], red[i]
                    p_ = slot[:, :, :].rearrange("p (t h) s -> p t (h s)", t=TB)[:, :, c0:c1]
                    dve.tensor_tensor(ang[i], p_.unsqueeze(3).to_broadcast([P, TB, c1 - c0, HALF]),
                                      freq[:, :].unsqueeze(1).unsqueeze(1).to_broadcast([P, TB, c1 - c0, HALF]),
                                      ALU.mult).then_inc(S["ang_mul"], 1)
                    dve.wait_ge(S["ang_mul"], n)
                    dve.tensor_scalar(r_, a_, float(1 / (2 * np.pi)), MAGIC, ALU.mult, ALU.add
                                      ).then_inc(S["ang_k"], 1)
                    dve.wait_ge(S["ang_k"], n)
                    dve.tensor_scalar(r_, r_, MAGIC, None, ALU.subtract).then_inc(S["ang_n"], 1)
                    dve.wait_ge(S["ang_n"], n)
                    dve.scalar_tensor_tensor(a_, r_, -TWO_PI_HI, a_, ALU.mult, ALU.add).then_inc(S["ang_r1"], 1)
                    dve.wait_ge(S["ang_r1"], n)
                    dve.scalar_tensor_tensor(a_, r_, -TWO_PI_LO, a_, ALU.mult, ALU.add).then_inc(S["ang_r2"], 1)
                    dve.wait_ge(S["ang_r2"], n)
                    dve.tensor_scalar(a_, a_, PI_CLAMP, -PI_CLAMP, ALU.min, ALU.max).then_inc(S["ang_clamp"], 1)

                for i in range(len(chunks)):
                    angles(i)
                    if i == 0:
                        dve.wait_ge(S["sel_cp"], (b + 1) * 4)
                        for tb in range(TB):
                            diagonals(b, 0, tb)
                high(b, 0, 0)
                double(b, 0, 0)
                dve.wait_ge(S["mk_ev"], (b + 1) * 2)
                query_masks(b, 0, 0)
                dve.wait_ge(S["l_exp"], b + 1)
                for i, v in enumerate((sA, sB)):
                    dve.tensor_tensor(PR[:, :, :, i, :], ew[:, :, :, :], v, ALU.mult).then_inc(S["pr_w"], 1)
                dve.wait_ge(S["pr_w"], (b + 1) * 2)
                dve.tensor_reduce(es[:, :, :], prod[:, :, :, :], AX_X, ALU.add).then_inc(S["es_done"], 1)
                dve.wait_ge(S["es_done"], b + 1)
                dve.tensor_tensor(lmax[:, 1, :], es[:, :, 0], es[:, :, 1], ALU.add).then_inc(S["es_sum"], 1)
                dve.wait_ge(S["es_sum"], b + 1)
                dve.reciprocal(lmax[:, 0, :], lmax[:, 1, :]).then_inc(S["l_rec"], 1)
                dve.wait_ge(S["l_rec"], b + 1)
                dve.tensor_tensor(wslot[:, :, :, :].rearrange("p t h s -> p (t h) s"), es[:, :, :],
                                  lmax[:, 0, :].unsqueeze(2).to_broadcast([P, TB * H, 2]), ALU.mult
                                  ).then_inc(S["w_done"], 1)
                for tb in range(2):
                    keep_kl(b, 0, 0, tb)
                with dve.Fori(0, PAIRS // 2) as hq:
                    for v in range(4):
                        hp, u, h = hq * 2 + v // 2, v % 2, hq * 4 + v
                        for s in range(TB):
                            g, w = s % 2, (s + 1) * P
                            uh, uu, tb = unit_at(h, u, s)
                            last = (h, s - 1) if s else (h - 1, TB - 1)
                            weigh = not (v == 0 and s == 0)
                            row_max(b, h, s, 0)
                            if weigh:
                                inverse_sums(b, *last)
                            diagonals(b, h + 1, s)
                            if weigh:
                                coefficients(b, *last)
                            row_max(b, h, s, 1)
                            if s == 1:
                                double(b, h + 1, 1 - u)
                            if weigh:
                                weigh_a(b, *last)
                            keep_kl(b, uh, uu, tb)
                            if weigh:
                                weigh_b(b, *last)
                            if s == 0:
                                high(b, h + 1, 1 - u)
                            if s == 1:
                                query_masks(b, h + 1, 1 - u)
                    inverse_sums(b, h, TB - 1)
                    coefficients(b, h, TB - 1)
                    weigh_a(b, h, TB - 1)
                    weigh_b(b, h, TB - 1)
                dve.wait_ge(S["att_t"], b + 1)
                dve.tensor_tensor(xb[:, :, :], psY[:, :].rearrange("p (t d) -> p t d", t=TB), xb[:, :, :], ALU.add
                                  ).then_inc(S["x1_done"], 1)
                dve.wait_ge(S["x1_done"], b + 1)
                layer_norm(b * 2 + 1)
                dve.tensor_copy(x1[:, bass.ds(b * TB, TB), :], xb[:, :, :]).then_inc(S["x1_kept"], 1)
                dve.wait_ge(S["h2_copy"], b + 1)
                h2b = h2[:, :, bass.ds(b * T, T)]
                dve.tensor_tensor(h2b[:, 1, :], hT[:, :], h2b[:, 0, :], ALU.subtract).then_inc(S["h2_low"], 1)
                dve.wait_ge(S["r_mm"], b + 1)
                dve.tensor_copy(rl[:, :, :].rearrange("p t e -> p (t e)"), psT0[:, 0:TB * E]).then_inc(S["r_ev"], 1)
                dve.wait_ge(S["r_ev"], b + 1)
                dve.tensor_reduce(rm[:, 0, :], rl[:, :, :], AX_X, ALU.max).then_inc(S["r_max"], 1)
                dve.wait_ge(S["r_max"], b + 1)
                top = rm[:, 0, :].unsqueeze(2).to_broadcast([P, TB, E])
                dve.tensor_tensor(rr[:, 0, :, :], rl[:, :, :], top, ALU.subtract).then_inc(S["r_sub"], 1)
                dve.tensor_tensor(rr[:, 1, :, :], rl[:, :, :], top, ALU.is_ge).then_inc(S["r_eq"], 1)
                dve.wait_ge(S["r_eq"], b + 1)
                dve.tensor_tensor(rr[:, 2, :, :], rr[:, 1, :, :], rank8[:, :].unsqueeze(1).to_broadcast([P, TB, E]),
                                  ALU.mult).then_inc(S["r_rk"], 1)
                dve.wait_ge(S["r_rk"], b + 1)
                dve.tensor_reduce(rm[:, 1, :], rr[:, 2, :, :], AX_X, ALU.max).then_inc(S["r_rm"], 1)
                dve.wait_ge(S["r_exp"], b + 1)
                dve.tensor_reduce(rm[:, 2, :], rr[:, 0, :, :], AX_X, ALU.add).then_inc(S["r_sum"], 1)
                dve.wait_ge(S["r_sum"], b + 1)
                dve.reciprocal(rm[:, 3, :], rm[:, 2, :]).then_inc(S["r_rec"], 1)
                dve.wait_ge(S["r_rm"], b + 1)
                dve.tensor_tensor(rr[:, 1, :, :], rr[:, 2, :, :], rm[:, 1, :].unsqueeze(2).to_broadcast([P, TB, E]),
                                  ALU.is_equal).then_inc(S["r_c"], 1)
                dve.wait_ge(S["r_c"], b * 2 + 1)
                dve.wait_ge(S["r_rec"], b + 1)
                dve.scalar_tensor_tensor(rr[:, 3, :, :], rr[:, 1, :, :], 2.0,
                                         rm[:, 3, :].unsqueeze(2).to_broadcast([P, TB, E]), ALU.mult, ALU.mult
                                         ).then_inc(S["r_c"], 1)
                dve.wait_ge(S["r_c"], b * 2 + 2)
                dve.tensor_copy(ecoef[:, bass.ds(b * TB, TB), :], rr[:, 3, :, :]).then_inc(S["r_cev"], 1)

            for t_ in range(B):
                dve.wait_ge(S["r_cT"], t_ + 1)
                dve.tensor_copy(coefT[:, t_ * T:(t_ + 1) * T], bank[4 + t_][0:E, :]).then_inc(S["r_cTev"], 1)
            dve.sem_inc(S["hid_done"], 1)

            def coef_row(m):
                dve.wait_ge(S["bc_mm"], (m - 1) * 4)
                dve.wait_ge(S["r_cTev"], B)
                dve.tensor_scalar(crow[:, :], coefT[:, :], ident[0:E, bass.ds(m - 1, 1)] if not isinstance(m, int)
                                  else ident[0:E, m - 1:m], None, ALU.mult).then_inc(S["crow_done"], 1)

            def hidden_and_sum(m, shared):
                n0 = m * 16
                if not shared:
                    coef_row(m)

                def total(m, t_, shared):
                    o = t_ % 2
                    dst = ffnT[:, t_ * 512:(t_ + 1) * 512]
                    dve.wait_ge(S["down_mm"], m * 4 + t_ + 1)
                    if shared:
                        dve.tensor_copy(dst, bank[4 + o][:, :]).then_inc(S["ffn_acc"], 1)
                        return
                    dve.wait_ge(S["bc_mm"], (m - 1) * 4 + t_ + 1)
                    dve.tensor_copy(bc[o][:, :], bank[6 + o][:, :]).then_inc(S["bc_ev"], 1)
                    dve.wait_ge(S["bc_ev"], (m - 1) * 4 + t_ + 1)
                    dve.tensor_tensor(wtd[o][:, :], bank[4 + o][:, :], bc[o][:, :], ALU.mult
                                      ).then_inc(S["wtd_done"], 1)
                    dve.wait_ge(S["wtd_done"], (m - 1) * 4 + t_ + 1)
                    dve.wait_ge(S["ffn_acc"], m * 4 + t_ - 3)
                    dve.tensor_tensor(dst, dst, wtd[o][:, :], ALU.add).then_inc(S["ffn_acc"], 1)

                def low_hidden(n, i):
                    dve.wait_ge(S["hid_hi"], n + 1)
                    dve.tensor_tensor(hid16[i][:, 1, :], hidden[i][:, :], hid16[i][:, 0, :], ALU.subtract
                                      ).then_inc(S["hid_lo"], 1)

                for i in range(16):
                    if not (shared and i == 0):
                        low_hidden(n0 + i - 1, (i - 1) % 2)
                    if not (shared and i < 2):
                        dve.wait_ge(S["hid_lo"], n0 + i - 1)
                    dve.wait_ge(S["silu_done"], n0 + i + 1)
                    dve.tensor_tensor(hidden[i % 2][:, :], bank[2 + i % 2][:, :], gateb[i % 2][:, :],
                                      ALU.mult).then_inc(S["hid_done"], 1)
                    if i % 4 == 2 and i > 2:
                        total(m, i // 4 - 1, shared)
                    if i == 2 and not shared:
                        total(m - 1, 3, isinstance(m, int) and m == 1)
                return low_hidden, total

            hidden_and_sum(0, True)
            hidden_and_sum(1, False)
            with dve.Fori(0, 3) as r:
                hidden_and_sum(r * 2 + 2, False)
                low_hidden, total = hidden_and_sum(r * 2 + 3, False)
            low_hidden(127, 1)
            total(7, 3, False)
            for b in range(B):
                dve.wait_ge(S["fin_t"], b + 1)
                dve.tensor_tensor(x1[:, b * TB:(b + 1) * TB, :],
                                  bank[b % 2][:, :].rearrange("p (t d) -> p t d", t=TB),
                                  x1[:, b * TB:(b + 1) * TB, :], ALU.add).then_inc(S["fin_done"], 1)

        @block.tensor
        def _(pe):
            pe.wait_ge(S["c_silu"], 1)
            pe.wait_ge(S["loaded"], 16 * 9)
            for j in range(6):
                mm = pe.matmul(psT0[:, j * B:(j + 1) * B], w_mod[:, j * DIM:(j + 1) * DIM], c_s[:, :],
                               start=True, stop=True)
            mm.then_inc(S["mod_mm"], 1)
            pe.wait_ge(S["ident_done"], 7)
            pe.wait_ge(S["init_done"], 11)

            def norm_rows(turn):
                pe.wait_ge(S["xn_done"], (turn + 1) * TB)
                for tb in range(TB):
                    mm = pe.transpose(psPT[:, tb * P:(tb + 1) * P], xn[:, tb, :], ident[:, :])
                mm.then_inc(S["xn_t"], 1)

            def sort_q(b, h, u, tb):
                m, r = unit_no(b, h, tb), rot_no(b, h)
                pe.wait_ge(S["lo_done"], 1 + r * 2 + 2)
                pe.wait_ge(S["diag_done"], r * 4 + tb + 1)
                pe.wait_ge(S["t_ev"], 1 + m * 3)
                pe.matmul(psT0[:, 0:3 * P], tile[:, u, tb, 0, 0:2, :].rearrange("p k c -> p (k c)"),
                          diag[:, tb, 0:3, :].rearrange("p j c -> p (j c)"), start=True, stop=True
                          ).then_inc(S["t_done"], 1)
                pe.wait_ge(S["kl_ev"], 1 + m)
                pe.matmul(psT1[:, 0:3 * P], tile[:, u, tb, 1, 0:2, :].rearrange("p k c -> p (k c)"),
                          diag[:, tb, 3:6, :].rearrange("p j c -> p (j c)"), start=True, stop=True
                          ).then_inc(S["t_done"], 1)

            def sort_k(b, h, u, tb):
                m = unit_no(b, h, tb)
                pe.wait_ge(S["dup_done"], rot_no(b, h) + 1)
                for i, (dst, k0, k1) in enumerate(((psT0, 2, 4), (psT1[0:HD, :], 4, 5))):
                    pe.wait_ge(S["t_ev"], 1 + m * 3 + i + 1)
                    kA, kB = [tile[:, u, tb, j, k0:k1, :].rearrange("p k c -> p (k c)") for j in range(2)]
                    d = diag[:, tb, :, :].rearrange("p j c -> p (j c)")
                    pe.matmul(dst[:, 0:3 * P], kA, d[:, 0:3 * P], start=True, stop=False)
                    pe.matmul(dst[:, P:3 * P], kB, d[:, 3 * P:5 * P], start=False, stop=True)
                    pe.matmul(dst[:, 3 * P:4 * P], kB, d[:, 5 * P:6 * P], start=True, stop=True
                              ).then_inc(S["t_done"], 1)

            def scores(b, h, u, s, e):
                m = unit_no(b, h, s)
                g, w = s % 2, (s + 1) * P
                pe.wait_ge(S["t_ev"], 1 + m * 3 + 3)
                pe.wait_ge(S["kl_ev"], 1 + m + 1)
                pe.wait_ge(S["mq_done"], rot_no(b, h) + 1)
                rows = slice(s * P, (s + 1) * P)
                o = psS[2 * g + e]
                pe.wait_ge(S["exp_done"], 1 + step_no(b, h, s) * 2 + e)
                for j in range(3):
                    q, n = qT[:, 3 * e + j, rows], e + j
                    pe.matmul(o[:, 0:w], q, kT[:, u, n, 0:w], start=(j == 0), stop=False)
                    pe.matmul(o[:, 0:w], q[0:HD, :], klT[0:HD, u, n, 0:w], start=False, stop=False)
                pe.matmul(o[:, 0:w], mq[0:HD + 1, u, e, rows], mkq[0:HD + 1, 0, 0:w], start=False, stop=False)
                pe.matmul(o[:, s * P:w], identbig[:, :], causal[:, :], start=False, stop=True
                          ).then_inc(S["scores_done"], 1)

            def prob_rows(b, h, u, ib):
                pe.wait_ge(S["acc_done"], 3 + step_no(b, h, ib) * 2 + 2)
                pe.wait_ge(S["pt_ev"], 1 + pt_no(b, h, ib))
                for jb in range(ib + 1):
                    mm = pe.transpose(psPT[:, jb * P:(jb + 1) * P], acc[ib % 2][:, jb * P:(jb + 1) * P], ident[:, :])
                mm.then_inc(S["pt_done"], 1)

            def values(b, hp):
                pe.wait_ge(S["pt_ev"], 1 + b * PTS_PER_B + hp * 8 + 2)
                pe.wait_ge(S["vb_done"], 1 + b * PAIRS + hp)
                pe.wait_ge(S["y_ev"], 1 + b * (PAIRS + 1) + hp)
                for jb in range(TB):
                    for u in range(2):
                        mm = pe.matmul(psY[u * HD:(u + 1) * HD, jb * P:T], v_b[:, jb, :], accT[u][:, jb, jb * P:T],
                                       start=(jb == 0), stop=(jb == TB - 1))
                mm.then_inc(S["pv_done"], 1)

            with pe.Fori(0, B) as b:
                norm_rows(b * 2)
                pe.wait_ge(S["h_ready"], b * 2 + 1)
                for tb in range(TB):
                    mm = pe.matmul(bank[3][:, tb * 64:(tb + 1) * 64], hT[:, tb * P:(tb + 1) * P], w_r[:, :],
                                   start=True, stop=True)
                mm.then_inc(S["lg_mm"], 1)
                for tb in range(TB):
                    if tb >= 2:
                        pe.wait_ge(S["qkv_ev"], (b * TB + tb - 1) * 3)
                    for j, i in enumerate((0, 1, 2) if tb % 2 == 0 else (4, 5, 7)):
                        mm = pe.matmul(bank[i][:, :], hT[:, tb * P:(tb + 1) * P], w_qkv[:, j * 512:(j + 1) * 512],
                                       start=True, stop=True)
                    mm.then_inc(S["proj_mm"], 1)
                    if tb == 0:
                        pe.wait_ge(S["mem16"], b + 1)
                        for to in range(TB):
                            for ti in range(to + 1):
                                mm = pe.matmul(psPT[:, to * 64:(to + 1) * 64], before[:, :] if ti == to else ones16[:, :],
                                               member16[:, ti, :, :].rearrange("p h n -> p (h n)"),
                                               start=(ti == 0), stop=(ti == to))
                        mm.then_inc(S["pos_mm"], 1)
                pe.wait_ge(S["sel_cp"], (b + 1) * 4)
                pe.wait_ge(S["qkv_ev"], (b + 1) * TB * 3)
                pe.sem_inc(S["pe_passed"], 1)
                for tb in range(TB):
                    for dst, o, src in ((psT16[0], 0, member16[:, tb, :, :].rearrange("p h n -> p (h n)")),
                                        (psT16[0], T, sel16[:, 0, tb, :]), (psT16[1], 0, sel16[:, 1, tb, :])):
                        mm = pe.transpose(dst[0:HD, o + tb * P:o + (tb + 1) * P], src, ident16[:, :])
                mm.then_inc(S["mk_t"], 1)
                pe.wait_ge(S["mk_ev"], (b + 1) * 2)
                for tb in range(2):
                    sort_q(b, 0, 0, tb)
                    sort_k(b, 0, 0, tb)
                with pe.Fori(0, PAIRS // 2) as hq:
                    for v in range(4):
                        hp, u, h = hq * 2 + v // 2, v % 2, hq * 4 + v
                        for s in range(TB):
                            uh, uu, tb = unit_at(h, u, s)
                            scores(b, h, u, s, 0)
                            if u == 0 and s == 2:
                                values(b, hp)
                            sort_q(b, uh, uu, tb)
                            scores(b, h, u, s, 1)
                            prob_rows(b, *rows_at(h, u, s))
                            sort_k(b, uh, uu, tb)
                prob_rows(b, H - 1, 1, 2)
                prob_rows(b, H - 1, 1, 3)
                values(b, PAIRS)
                pe.wait_ge(S["y_ev"], 1 + (b + 1) * (PAIRS + 1))
                for i in range(PAIRS):
                    mm = pe.matmul(psPT[:, :], w_o[:, i, :], yT[:, i + 1, :], start=(i == 0), stop=(i == PAIRS - 1))
                mm.then_inc(S["wo_mm"], 1)
                pe.wait_ge(S["att_ev"], b + 1)
                for tb in range(TB):
                    mm = pe.transpose(psY[:, tb * P:(tb + 1) * P], att[:, tb * P:(tb + 1) * P], ident[:, :])
                mm.then_inc(S["att_t"], 1)
                norm_rows(b * 2 + 1)
                pe.wait_ge(S["h_ready"], b * 2 + 2)
                for tb in range(TB):
                    mm = pe.matmul(psT0[:, tb * E:(tb + 1) * E], hT[:, tb * P:(tb + 1) * P], w_rt[:, :],
                                   start=True, stop=True)
                mm.then_inc(S["r_mm"], 1)
            pe.wait_ge(S["h2_low"], B)
            pe.wait_ge(S["r_cev"], B)
            for t_ in range(B):
                for tb in range(TB):
                    mm = pe.transpose(bank[4 + t_][0:E, tb * P:(tb + 1) * P], ecoef[:, t_ * TB + tb, :], ident[:, :])
                mm.then_inc(S["r_cT"], 1)

            def products(dst, w, k, c_, rhs, start, stop):
                for j, (wl, rl_) in enumerate(((0, 0), (0, 1), (1, 0))):
                    mm = pe.matmul(dst, w[:, wl, k, c_ * P:(c_ + 1) * P], rhs[rl_],
                                   start=(start and j == 0), stop=(stop and j == 2))
                return mm

            def ffn(m, slot_, shared):
                n0 = m * 16
                pe.wait_ge(S["w_lo"], m + 1)

                def gate_up(i):
                    t_, c_ = i // 4, i % 4
                    if not (shared and i < 2):
                        pe.wait_ge(S["silu_done"], n0 + i - 1)
                        pe.wait_ge(S["hid_done"], n0 + i)
                    rhs = [h2[:, l, t_ * 512:(t_ + 1) * 512] for l in range(2)]
                    products(bank[i % 2][:, :], w_hl[slot_], 1, c_, rhs, True, True)
                    products(bank[2 + i % 2][:, :], w_hl[slot_], 0, c_, rhs, True, True).then_inc(S["gu_mm"], 1)

                def down(m, i, slot_, shared):
                    t_, c_ = i // 4, i % 4
                    o = t_ % 2
                    if c_ == 0:
                        if not (shared and t_ < 2):
                            pe.wait_ge(S["ffn_acc"], m * 4 + t_ - 1)
                        if not shared:
                            pe.wait_ge(S["crow_done"], m)
                            pe.matmul(bank[6 + o][:, :], ones8[:, :], crow[:, t_ * 512:(t_ + 1) * 512],
                                      start=True, stop=True).then_inc(S["bc_mm"], 1)
                    pe.wait_ge(S["hid_lo"], m * 16 + i + 1)
                    products(bank[4 + o][:, :], w_hl[slot_], 2, c_, [hid16[i % 2][:, l, :] for l in range(2)],
                             c_ == 0, c_ == 3).then_inc(S["hid_used"], 1)
                    if c_ == 3:
                        pe.wait_ge(S["hid_used"], m * 16 + i + 1)
                        pe.sem_inc(S["down_mm"], 1)

                for i in range(16):
                    gate_up(i)
                    if i >= 2:
                        down(m, i - 2, slot_, shared)
                    elif not shared:
                        down(m - 1, 14 + i, 1 - slot_, isinstance(m, int) and m == 1)
                return down

            ffn(0, 0, True)
            ffn(1, 1, False)
            with pe.Fori(0, 3) as r:
                ffn(r * 2 + 2, 0, False)
                down = ffn(r * 2 + 3, 1, False)
            for i in (14, 15):
                down(7, i, 1, False)
            for b in range(B):
                pe.wait_ge(S["fin_g"], b + 1)
                if b >= 2:
                    pe.wait_ge(S["fin_done"], b - 1)
                for tb in range(TB):
                    mm = pe.transpose(bank[b % 2][:, tb * P:(tb + 1) * P],
                                      ffnT[:, b * T + tb * P:b * T + (tb + 1) * P], ident[:, :])
                mm.then_inc(S["fin_t"], 1)


_INS = ['L0_attn_x', 'L0_attn_wq', 'L0_attn_wk', 'L0_attn_wv', 'L0_attn_wr', 'L0_attn_wo', 'L0_ffn_w_router',
        'L0_ffn_w_up', 'L0_ffn_w_gate', 'L0_ffn_w_down', 'L0_ffn_ws_up', 'L0_ffn_ws_gate', 'L0_ffn_ws_down',
        'L0_c', 'L0_wmod']
_OUTS = [((B, T, DIM), 'float32')]


def _rotary_frequencies():
    e = np.arange(0, HD, 2, dtype=np.float32) / np.float32(HD)
    f = np.float32(1.0) / np.power(np.float32(10000.0), e, dtype=np.float32)
    return np.ascontiguousarray(np.broadcast_to(f.astype(np.float32), (P, HALF)))


def kernel(**inputs):
    import numpy as _np
    import concourse.bacc as _bacc
    from concourse import mybir as _mybir
    from concourse.bass_utils import run_bass_kernel_spmd as _run

    nc = _bacc.Bacc("TRN2", target_bir_lowering=False, num_devices=1)
    arrays, args = {}, []
    for name in _INS:
        a = _np.ascontiguousarray(inputs[name])
        arrays[f"in_{name}_dram"] = a
        args.append(nc.dram_tensor(f"in_{name}_dram", a.shape, _mybir.dt.from_np(a.dtype), kind="ExternalInput").ap())
    f = _rotary_frequencies()
    arrays["rotary_frequencies_dram"] = f
    args.append(nc.dram_tensor("rotary_frequencies_dram", f.shape, _mybir.dt.from_np(f.dtype), kind="ExternalInput").ap())
    for i, (shape, dtype) in enumerate(_OUTS):
        dt = _mybir.dt.from_np(_np.dtype(dtype))
        args.append(nc.dram_tensor(f"out_{i}_dram", shape, dt, kind="ExternalOutput").ap())
    block_kernel(nc, *args)
    r = _run(nc, [arrays], core_ids=[0])
    got = tuple(r.results[0][f"out_{i}_dram"] for i in range(len(_OUTS)))
    return got[0]
```
